# Optimizing a Trainium2 kernel written in Bass

```python
import numpy as np
import jax
import jax.numpy as jnp

def _softmax(x, axis=-1):
    return jax.nn.softmax(x, axis=axis)

def _gelu(x):
    return jax.nn.gelu(x, approximate=True)

def _silu(x):
    return jax.nn.silu(x)

def _sigmoid(x):
    return jax.nn.sigmoid(x)

def _layernorm(x, axis=-1, eps=1e-05):
    m = jnp.mean(x, axis=axis, keepdims=True)
    v = jnp.var(x, axis=axis, keepdims=True)
    return (x - m) / jnp.sqrt(v + eps)

def _scatter_add(tgt, idx, src, axis=0):
    return tgt.at[idx].add(src)

def _segment_sum(src, seg, n):
    return jax.ops.segment_sum(src, seg, n)
kernel_name = 'mk_seq_postln_d1_jaxref_r8_f984d6'

def setup_inputs(seed: int=0):
    np.random.seed(seed)
    _w = jnp.asarray

    def _L0_attn_setup():
        import jax, jax.numpy as jnp
        import numpy as np
        B, T, C = (2, 256, 128)
        NH = 16
        HD = C // NH

        def build_alibi_bias(n_head, max_len):
            slopes = jnp.arange(1, n_head + 1, dtype=jnp.float32) / n_head
            ar = jnp.arange(max_len, dtype=jnp.float32)
            return slopes[:, None, None] * (ar[None, None, :] - ar[None, :, None])
        key = jax.random.key(seed)
        ks = jax.random.split(key, 7)
        s = 0.02
        return {'x': jax.random.normal(ks[0], (B, T, C), dtype=jnp.float32), 'q_w': jax.random.normal(ks[1], (C, C), dtype=jnp.float32) * s, 'q_b': jnp.zeros((C,), dtype=jnp.float32), 'kv_w': jax.random.normal(ks[2], (C, 2 * C), dtype=jnp.float32) * s, 'kv_b': jnp.zeros((2 * C,), dtype=jnp.float32), 'o_w': jax.random.normal(ks[3], (C, C), dtype=jnp.float32) * s, 'o_b': jnp.zeros((C,), dtype=jnp.float32)}
    _L0_attn_in = _L0_attn_setup()

    def _L0_ffn_setup():
        import jax, jax.numpy as jnp
        import numpy as np
        TOP_K = 2

        def _ffn(x, gw, uw, dw):
            return jax.nn.silu(x @ gw.T) * (x @ uw.T) @ dw.T
        key = jax.random.key(seed)
        ks = jax.random.split(key, 8)
        w = lambda k, shape: jax.random.normal(k, shape, jnp.float32) * 0.02
        return dict(x=jax.random.normal(ks[0], (4, 256, 128), jnp.float32), gate_w=w(ks[1], (8, 128)), expert_gate=w(ks[2], (8, 352, 128)), expert_up=w(ks[3], (8, 352, 128)), expert_down=w(ks[4], (8, 128, 352)), shared_gate=w(ks[5], (352, 128)), shared_up=w(ks[6], (352, 128)), shared_down=w(ks[7], (128, 352)))
    _L0_ffn_in = _L0_ffn_setup()
    _d = {'L0_attn_x': _L0_attn_in['x'], 'L0_attn_q_w': _L0_attn_in['q_w'], 'L0_attn_q_b': _L0_attn_in['q_b'], 'L0_attn_kv_w': _L0_attn_in['kv_w'], 'L0_attn_kv_b': _L0_attn_in['kv_b'], 'L0_attn_o_w': _L0_attn_in['o_w'], 'L0_attn_o_b': _L0_attn_in['o_b'], 'L0_ffn_gate_w': _L0_ffn_in['gate_w'], 'L0_ffn_expert_gate': _L0_ffn_in['expert_gate'], 'L0_ffn_expert_up': _L0_ffn_in['expert_up'], 'L0_ffn_expert_down': _L0_ffn_in['expert_down'], 'L0_ffn_shared_gate': _L0_ffn_in['shared_gate'], 'L0_ffn_shared_up': _L0_ffn_in['shared_up'], 'L0_ffn_shared_down': _L0_ffn_in['shared_down']}
    _x0 = _d['L0_attn_x']
    _d['L0_attn_x'] = jax.random.normal(jax.random.fold_in(jax.random.key(seed), 1), (16, 512, 128), dtype=_x0.dtype)
    del _x0
    return _d

def reference(L0_attn_x, L0_attn_q_w, L0_attn_q_b, L0_attn_kv_w, L0_attn_kv_b, L0_attn_o_w, L0_attn_o_b, L0_ffn_gate_w, L0_ffn_expert_gate, L0_ffn_expert_up, L0_ffn_expert_down, L0_ffn_shared_gate, L0_ffn_shared_up, L0_ffn_shared_down):

    def _L0_attn_ref(x, q_w, q_b, kv_w, kv_b, o_w, o_b):
        import jax, jax.numpy as jnp
        import numpy as np
        B, T, C = (2, 256, 128)
        NH = 16
        HD = C // NH

        def build_alibi_bias(n_head, max_len):
            slopes = jnp.arange(1, n_head + 1, dtype=jnp.float32) / n_head
            ar = jnp.arange(max_len, dtype=jnp.float32)
            return slopes[:, None, None] * (ar[None, None, :] - ar[None, :, None])
        Bx, Tx, Cx = x.shape
        q = (x @ q_w + q_b).reshape(Bx, Tx, NH, HD).transpose(0, 2, 1, 3)
        kv = (x @ kv_w + kv_b).reshape(Bx, Tx, 2, NH, HD).transpose(2, 0, 3, 1, 4)
        k, v = (kv[0], kv[1])
        att = jnp.einsum('bhqd,bhkd->bhqk', q, k) * (1.0 / np.sqrt(HD))
        att = att + build_alibi_bias(NH, Tx)[None]
        causal = jnp.tril(jnp.ones((Tx, Tx), dtype=bool))
        att = jnp.where(causal[None, None], att, -jnp.inf)
        att = jax.nn.softmax(att, axis=-1)
        y = jnp.einsum('bhqk,bhkd->bhqd', att, v)
        y = y.transpose(0, 2, 1, 3).reshape(Bx, Tx, Cx)
        return y @ o_w + o_b

    def _L0_ffn_ref(x, gate_w, expert_gate, expert_up, expert_down, shared_gate, shared_up, shared_down):
        import jax, jax.numpy as jnp
        import numpy as np
        TOP_K = 2

        def _ffn(x, gw, uw, dw):
            return jax.nn.silu(x @ gw.T) * (x @ uw.T) @ dw.T
        B, S, H = x.shape
        xf = x.reshape(-1, H)
        T = xf.shape[0]
        E = expert_gate.shape[0]
        shared = _ffn(xf, shared_gate, shared_up, shared_down)
        logits = xf @ gate_w.T
        probs = jax.nn.softmax(logits, axis=-1)
        topw, topi = jax.lax.top_k(probs, TOP_K)
        topw = topw / (topw.sum(-1, keepdims=True) + 1e-20)
        comb = jnp.zeros((T, E), xf.dtype).at[jnp.arange(T)[:, None], topi].add(topw)

        def body(acc, ws):
            gw, uw, dw, wcol = ws
            return (acc + _ffn(xf, gw, uw, dw) * wcol[:, None], None)
        routed, _ = jax.lax.scan(body, jnp.zeros_like(xf), (expert_gate, expert_up, expert_down, comb.T))
        return (shared + routed).reshape(B, S, H)
    x = L0_attn_x
    x = _layernorm(x + _L0_attn_ref(x, L0_attn_q_w, L0_attn_q_b, L0_attn_kv_w, L0_attn_kv_b, L0_attn_o_w, L0_attn_o_b), axis=-1)
    x = _layernorm(x + _L0_ffn_ref(x, L0_ffn_gate_w, L0_ffn_expert_gate, L0_ffn_expert_up, L0_ffn_expert_down, L0_ffn_shared_gate, L0_ffn_shared_up, L0_ffn_shared_down), axis=-1)
    return x

_drawn_inputs = setup_inputs


def setup_inputs(seed=0):
    import zlib

    import numpy as np

    out = dict(_drawn_inputs(seed))
    spreads = {'L0_attn_q_b': (0.0, 0.8), 'L0_attn_kv_b': (0.0, 0.351), 'L0_attn_o_b': (0.0, 0.1)}
    factors = {'L0_attn_q_w': 8.0,
     'L0_ffn_gate_w': 8.0,
     'L0_ffn_expert_gate': 8.0,
     'L0_ffn_expert_up': 8.0,
     'L0_ffn_expert_down': 8.0,
     'L0_ffn_shared_gate': 5.908,
     'L0_ffn_shared_up': 5.853,
     'L0_ffn_shared_down': 5.877}
    for name, (base, spread) in spreads.items():
        noise = np.random.default_rng([zlib.crc32(name.encode()), seed]).standard_normal(out[name].shape)
        drawn = base * np.exp(spread * noise) if base else spread * noise
        out[name] = jnp.asarray(drawn.astype(out[name].dtype))
    for name, factor in factors.items():
        out[name] = (out[name] * factor).astype(out[name].dtype)
    return out
```

```python
from contextlib import ExitStack

import concourse.bass as bass
import numpy as np
from concourse import mybir

F32 = mybir.dt.float32
BF16 = mybir.dt.bfloat16
I32 = mybir.dt.int32
U16 = mybir.dt.uint16
ALU = mybir.AluOpType
ACT = mybir.ActivationFunctionType
AX = mybir.AxisListType

P = 128
B, T, C = 16, 512, 128
NH, HD = 16, 8
QT = T // P
NTILE = B * QT
QUAD = 4
NQUAD = NH // QUAD
UNITS = 5
MAXB = 40
PARTS = 3
PROD = PARTS * PARTS * HD
BIAS_ROWS = 4
MAX_ROW = 96
STACK_ROWS = 128
VW = 32
SCALE = 1.0 / float(np.sqrt(HD))
NEG = -3.0e38
EPS = 1e-5


def bf16_bits(a):
    return (np.ascontiguousarray(a, np.float32).view(np.uint32) >> np.uint32(16)).astype(np.uint16)


def stack_constants():
    slope = np.arange(1, NH + 1, dtype=np.float32) / NH
    pos = slope[:, None] * np.arange(T, dtype=np.float32)[None, :]
    hi = (pos.view(np.uint32) & np.uint32(0xFFFF0000)).view(np.float32)
    q = np.zeros((STACK_ROWS - PROD, NH, T), np.float32)
    k = np.zeros((STACK_ROWS - PROD, NH, T), np.float32)
    q[0:2] = 1
    k[0], k[1] = hi, pos - hi
    q[2:4] = -k[0:2]
    k[2:4] = 1
    k[MAX_ROW - PROD:MAX_ROW - PROD + PARTS] = 1
    return bf16_bits(q), bf16_bits(k)


def causal_constants():
    mask = np.triu(np.full((P, P), NEG, np.float32), 1)
    return bf16_bits(np.stack([mask, mask.T]))


class Step:

    def __init__(self, number, parity, every):
        self.number, self.parity, self.every = number, parity, every

    def has(self, off):
        return self.every or 0 <= self.number + off < B

    def first(self, off):
        return not self.every and self.number + off == 0

    def at(self, off, per_seq, done):
        return (self.number + off) * per_seq + done

    def at_same(self, off, done):
        return (self.number + off - self.par(off)) * (done // 2) + done

    def par(self, off):
        return (self.parity + off) % 2


def segment(hh, kt):
    if kt == 0:
        return hh // 2, (hh % 2) * T, T
    if kt == 2:
        return 4, hh * 2 * P, 2 * P
    return 2 + hh // 2, (hh % 2) * T + (0 if kt == 1 else 3 * P), T - kt * P


MAX_SLOTS = (3, 3, 2, 0)
JOBS = (("xt", "q", "k", "qr", "kr"), ("y0", "y1", "y2", "y3", "v"), ("yn", "o", "x1t"), ("m", "lg"))


def plan(g):
    score = ["unit0", "unit1", "pv0", "unit2", "pv1", "unit3", "pv2", "unit4"]
    first = 5 * sum(MAX_SLOTS[:g])
    maxes = [f"max{first + n}" for n in range(5 * MAX_SLOTS[g])]
    jobs = list(JOBS[g])
    keyed = []
    for rank, items in enumerate((score, jobs, maxes)):
        lead = 0.5 if rank < 2 else 0.05
        keyed += [((n + lead) / len(items), rank, n, x) for n, x in enumerate(items)]
    if g == 3:
        keyed = [((-1.0, 0, 0, x) if x == "m" else (a, r, n, x)) for a, r, n, x in keyed]
    return [x for *_, x in sorted(keyed)]


READERS = {
    "xt": ("xT_ready", 1, 1), "q": ("qk_split", 4, 1), "k": ("qk_split", 4, 2),
    "y0": ("y_normed", 8, 2), "y1": ("y_normed", 8, 4), "y2": ("y_normed", 8, 6), "y3": ("y_normed", 8, 8),
    "v": ("v_ready", 1, 1), "yn": ("ynT_ready", 1, 1), "o": ("z_ready", 1, 1), "x1t": ("x1T_ready", 1, 1),
    "m": ("m_rest", 2, 1), "lg": ("logits_kept", 1, 1),
}
STAGE = {"xt": 2, "q": 2, "k": 2, "qr": 2, "kr": 2, "v": 1, "m": 1, "yn": -1, "o": -1, "x1t": -1, "lg": -1,
         "y0": -1, "y1": -1, "y2": -1, "y3": -1}
BANK_ORDER = [j for g in range(NQUAD) for j in plan(g) if j in READERS]


def bank_before(st, job):
    n = BANK_ORDER.index(job)
    for back in range(0, 3):
        order = BANK_ORDER[:n] if back == 0 else BANK_ORDER
        for j in reversed(order):
            if st.every or 0 <= st.number - back + STAGE[j] < B:
                return j, STAGE[j] - back
    return None


NE = 8
F = 352
FCH = [(j, min(P, F - j)) for j in range(0, F, P)]
NCH = len(FCH)
TURN = 4
CHUNKS = 2
CT = NTILE // CHUNKS
GROUPS = CHUNKS * NE
CSLOT = -(-(2 * CT + NE - 1) // TURN) * TURN
NSLOT = CHUNKS * CSLOT


def attention(nc, io, dram, keep):
    with ExitStack() as ctx:
        def sb(name, shape, dt=F32):
            return ctx.enter_context(nc.sbuf_tensor(name, shape, dt))

        def ps(name, cols=T):
            return ctx.enter_context(nc.psum_tensor(name, [P, cols], F32))

        def sem(name):
            return ctx.enter_context(nc.semaphore(name))

        ident = sb("ident", [P, P])
        identb = sb("identb", [P, P], BF16)
        causal = sb("causal", [P, 2, P], BF16)
        zeros = sb("zeros", [P, C])
        wkv_in = sb("wkv_in", [P, 2 * C])
        wq = sb("wq", [P, C])
        wk = sb("wk", [P, C])
        wo = sb("wo", [P, C])
        qb = sb("qb", [P, 1])
        qb_scaled = sb("qb_scaled", [P, 1])
        kb = sb("kb", [P, 1])
        vb = sb("vb", [P, C])
        ob = sb("ob", [P, C])
        gw = sb("gw", [P, 8])
        xin = [sb(f"xin{n}", [P, QT, C]) for n in range(2)]
        xT = [sb(f"xT{n}", [P, T]) for n in range(2)]
        qstack = [sb(f"qstack{n}", [P, NH, T], BF16) for n in range(2)]
        kstack = [sb(f"kstack{n}", [P, NH, T], BF16) for n in range(2)]
        vaug = [sb(f"vaug{n}", [P, QT, NH, VW]) for n in range(2)]
        yraw = [sb(f"yraw{n}", [P, NQUAD, T]) for n in range(2)]
        probs = [sb(f"probs{n}", [P, UNITS * 2 * T]) for n in range(2)]
        whole = [sb(n, [P, T]) for n in ("q_whole", "k_whole")]
        rest = [sb(n, [P, T]) for n in ("q_rest", "k_rest")]
        wq_in = rest[0][:, 0:C]
        parts = sb("parts", [P, 2, PARTS, T], BF16)
        maxA = sb("maxA", [P, NH, 4])
        maxB = sb("maxB", [P, NH, 4])
        maxC = sb("maxC", [P, NH, 2])
        rowmax = sb("rowmax", [P, NH, QT])
        mparts = sb("mparts", [NH * QT, PARTS, P], BF16)
        mrest = sb("mrest", [NH * QT, P])
        rsum = sb("rsum", [P, NH])
        ynorm = sb("ynorm", [P, QT, NH, HD])
        ynT = sb("ynT", [P, T])
        xres = sb("xres", [P, QT, C])
        stats = sb("stats", [P, QT, 6])
        mean_var = sb("mean_var", [P, QT, 2])
        rstd = sb("rstd", [P, QT])
        var_eps = sb("var_eps", [P, QT])
        minus_half = sb("minus_half", [P, QT])
        eps = sb("eps", [P, QT])
        x1_tiles = sb("x1_tiles", [P, QT, C])
        x1T = ynT

        scores = [ps(f"scores{n}", 2 * T) for n in range(2)]
        maxed = [ps(f"maxed{n}") for n in range(2)]
        pv = ps("pv")
        misc = ps("misc")

        names = """const_loaded const_ready unit_ready max_ready pv_ready xT_ps q_ps k_ps v_ps m_ps y_ps ynT_ps o_ps
            x1T_ps lg_ps exp_done xT_ready qk_high y_kept m_high ynT_ready x1T_ready max_taken rowmax_ready
            qk_split m_rest v_ready y_normed z_ready ln_done rstd_ready logits_kept zeros_set rows_zeroed qk_low res_biased x1_kept x_loaded0 x_loaded1 stats_passed maxima_passed
            xres_loaded parts_stored max_rows""".split()
        S = {n: sem(n) for n in names}
        n_const = [0]
        x_loaded = [S["x_loaded0"], S["x_loaded1"]]
        stack_loaded = [[sem(f"stack{n}_loaded{g}") for g in range(NQUAD)] for n in range(2)]

        def ready(eng, st, job):
            before = bank_before(st, job)
            if before:
                name, per, done = READERS[before[0]]
                eng.wait_ge(S[name], st.at(before[1], per, done))

        def steps(eng, body):
            for n in range(-3, 3):
                body(Step(n, n % 2, False))
            with eng.Fori(3, B - 4, 2) as n:
                body(Step(n, 1, True))
                body(Step(n + 1, 0, True))
            for n in (B - 3, B - 2, B - 1, B):
                body(Step(n, n % 2, False))

        with nc.Block() as block:

            @block.sync
            def _(sp):
                sp.wait_ge(S["zeros_set"], 1)

                def const(out, in_):
                    sp.dma_start(out, in_).then_inc(S["const_loaded"], 16)
                    n_const[0] += 16

                const(ident[:], io["ident"])
                const(identb[:].bitcast(U16), io["identb"])
                const(causal[:].bitcast(U16), io["causal"].rearrange("w p t -> p w t"))
                const(wq_in, io["q_w"])
                const(wkv_in[:], io["kv_w"])
                const(wo[:], io["o_w"])
                const(vb[:], io["kv_b"][C:2 * C].unsqueeze(0).to_broadcast([P, C]))
                const(ob[:], io["o_b"].unsqueeze(0).to_broadcast([P, C]))
                with nc.allow_non_contiguous_dma(reason="biases by (width, head), and the router's weights transposed"):
                    const(qb[:], io["q_b"].rearrange("(h d u) -> d h u", d=HD, u=1))
                    const(kb[:], io["kv_b"][0:C].rearrange("(h d u) -> d h u", d=HD, u=1))
                    const(gw[:], io["gate_w"].rearrange("e c -> c e"))
                for n in range(2):
                    const(qstack[n][PROD:, :, :].bitcast(U16), io["qstack_rows"])
                    const(kstack[n][PROD:, :, :].bitcast(U16), io["kstack_rows"])

                def load_stack(st, g):
                    src = dram["parts"][st.par(2)]
                    heads = slice(g * QUAD, (g + 1) * QUAD)
                    to_q, to_k = qstack[st.par(2)], kstack[st.par(2)]
                    rows = PARTS * HD
                    for a in range(PARTS):
                        sp.dma_start(to_q[a * rows:(a + 1) * rows, heads, :],
                                     src[0, a, :, heads, :].unsqueeze(0).to_broadcast([PARTS, HD, QUAD, T])
                                     .rearrange("c d h t -> c d (h t)")).then_inc(stack_loaded[st.par(2)][g], 16)
                    sp.dma_start(to_k[0:PROD, heads, :],
                                 src[1, :, :, heads, :].rearrange("a d h t -> (a d) (h t)").unsqueeze(0)
                                 .to_broadcast([PARTS, rows, QUAD * T])).then_inc(stack_loaded[st.par(2)][g], 16)

                def body(st):
                    if st.has(3):
                        if not st.first(3) and (st.every or st.number + 3 >= 2):
                            sp.wait_ge(S["xT_ps"], st.at(1, 1, 1))
                        sp.dma_start(xin[st.par(3)][:], io["x"][bass.ds(st.number + 3, 1)]
                                     .rearrange("b (i p) c -> p (b i) c", p=P)).then_inc(x_loaded[st.par(3)], 16)
                    if st.has(-1):
                        if not st.first(-1):
                            sp.wait_ge(S["z_ready"], st.at(-2, 1, 1))
                        sp.dma_start(xres[:], io["x"][bass.ds(st.number - 1, 1)]
                                     .rearrange("b (i p) c -> p (b i) c", p=P)).then_inc(S["xres_loaded"], 16)
                    if st.has(2):
                        sp.wait_ge(S["qk_low"], st.at(2, 2, 2))
                        sp.wait_ge(S["qk_high"], st.at(2, 4, 4))
                        sp.dma_start(dram["parts"][st.par(2)].rearrange("w a d h t -> (d h) (w a) t"),
                                     parts[:].rearrange("p w a t -> p (w a) t")).then_inc(S["parts_stored"], 16)
                        sp.wait_ge(S["parts_stored"], st.at(2, 16, 16))
                    if st.has(0):
                        rows, part = CSLOT * P // B, P // 2
                        for sorted_rows in dram["x_sorted"]:
                            sp.dma_start(sorted_rows[bass.ds(st.number * rows, rows), :]
                                         .rearrange("(n p) c -> p n c", p=part),
                                         zeros[0:part, :].unsqueeze(1).to_broadcast([part, rows // part, C])) \
                                .then_inc(S["rows_zeroed"], 16)
                    for g in range(NQUAD):
                        if g == 3 and st.has(1):
                            sp.wait_ge(S["m_rest"], st.at(1, 2, 2))
                            sp.wait_ge(S["m_high"], st.at(1, 2, 2))
                            for a in range(PARTS):
                                sp.dma_start(qstack[st.par(1)][MAX_ROW + a:MAX_ROW + a + 1, :, :]
                                             .rearrange("a h (i t) -> a (h i) t", t=P),
                                             mparts[:, a, :]).then_inc(S["max_rows"], 16)
                        if st.has(2):
                            if st.has(0):
                                sp.wait_ge(S["unit_ready"], st.at(0, 20, 5 * g + 5))
                            load_stack(st, g)

                steps(sp, body)
                sp.wait_ge(S["rows_zeroed"], 16 * B * CHUNKS)

            @block.tensor
            def _(pe):
                pe.wait_ge(S["const_loaded"], n_const[0])
                pe.wait_ge(S["const_ready"], 9)

                def transposes(srcs, done):
                    for n, src in enumerate(srcs):
                        last = pe.transpose(misc[0:src.shape[1], n * P:(n + 1) * P], src, ident[:])
                    last.then_inc(S[done], 1)

                def job(st, name):
                    ready(pe, st, name)
                    if name == "xt":
                        pe.wait_ge(x_loaded[st.par(2)], st.at_same(2, 16))
                        transposes([xin[st.par(2)][:, i, :] for i in range(QT)], "xT_ps")
                    elif name in ("q", "k"):
                        pe.wait_ge(S["xT_ready"], st.at(2, 1, 1))
                        w = wq if name == "q" else wk
                        pe.matmul(misc[:], w[:], xT[st.par(2)][:], start=True, stop=True).then_inc(S[name + "_ps"], 1)
                    elif name == "v":
                        for i in range(QT):
                            last = pe.matmul(misc[:, i * P:(i + 1) * P], xT[st.par(1)][:, i * P:(i + 1) * P],
                                             wkv_in[:, C:2 * C], start=True, stop=True)
                        last.then_inc(S["v_ps"], 1)
                    elif name == "m":
                        pe.wait_ge(S["rowmax_ready"], st.at(1, 4, 4))
                        pe.sem_inc(S["maxima_passed"], 1)
                        transposes([rowmax[:].rearrange("p h i -> p (h i)")], "m_ps")
                    elif name[0] == "y" and name[1] != "n":
                        i = int(name[1])
                        if i == 0:
                            pe.wait_ge(S["y_kept"], st.at(-1, 4, 4))
                        transposes([yraw[st.par(-1)][:, g, i * P:(i + 1) * P] for g in range(NQUAD)], "y_ps")
                    elif name == "yn":
                        pe.wait_ge(S["y_normed"], st.at(-1, 8, 8))
                        transposes([ynorm[:, i].rearrange("p h d -> p (h d)") for i in range(QT)], "ynT_ps")
                    elif name == "o":
                        pe.wait_ge(S["ynT_ready"], st.at(-1, 1, 1))
                        for i in range(QT):
                            last = pe.matmul(misc[:, i * P:(i + 1) * P], ynT[:, i * P:(i + 1) * P], wo[:],
                                             start=True, stop=True)
                        last.then_inc(S["o_ps"], 1)
                    elif name == "x1t":
                        pe.wait_ge(S["ln_done"], st.at(-1, 12, 12))
                        transposes([x1_tiles[:, i, :] for i in range(QT)], "x1T_ps")
                    elif name == "lg":
                        pe.wait_ge(S["x1T_ready"], st.at(-1, 1, 1))
                        for i in range(QT):
                            last = pe.matmul(misc[:, i * 8:(i + 1) * 8], x1T[:, i * P:(i + 1) * P], gw[:],
                                             start=True, stop=True)
                        last.then_inc(S["lg_ps"], 1)

                def max_bank(st, n):
                    pair, k = divmod(n, 5)
                    if k in (0, 2, 4):
                        head = 2 * pair + (k == 2) + (k == 4)
                        if k != 2 or head % QUAD == 0:
                            pe.wait_ge(stack_loaded[st.par(1)][head // QUAD], st.at_same(1, 64))
                    if n >= 2 or not st.first(1):
                        pe.wait_ge(S["max_taken"], st.at(1, MAXB, n - 1))
                    bank = maxed[n % 2]
                    q, ks = qstack[st.par(1)], kstack[st.par(1)]
                    if k == 4:
                        blocks = [(2 * pair, 1, 0), (2 * pair + 1, 1, 2 * P)]
                    elif k % 2 == 0:
                        blocks = [(2 * pair + k // 2, 3, 0)]
                    else:
                        blocks = [(2 * pair + k // 2, 2, 0), (2 * pair + k // 2, 0, 3 * P)]
                    for h, i, col in blocks:
                        pe.matmul(bank[:, col:col + (i + 1) * P], q[0:MAX_ROW, h, i * P:(i + 1) * P],
                                  ks[0:MAX_ROW, h, 0:(i + 1) * P], start=True, stop=False)
                        last = pe.matmul(bank[:, col + i * P:col + (i + 1) * P], identb[:], causal[:, 0, :],
                                         start=False, stop=True)
                    last.then_inc(S["max_ready"], 1)

                def unit(st, g, u):
                    n = 5 * g + u
                    if n == 0:
                        pe.wait_ge(S["max_rows"], st.at(0, 48, 48))
                    if n >= 2 or not st.first(0):
                        pe.wait_ge(S["exp_done"], st.at(0, 20, n - 1))
                    for hh in range(QUAD):
                        for kt in range(QT):
                            at, col, width = segment(hh, kt)
                            if at == u:
                                h = g * QUAD + hh
                                pe.matmul(scores[n % 2][:, col:col + width],
                                          kstack[st.par(0)][:, h, kt * P:(kt + 1) * P],
                                          qstack[st.par(0)][:, h, kt * P:T], start=True, stop=False)
                                last = pe.matmul(scores[n % 2][:, col:col + P], identb[:], causal[:, 1, :],
                                                 start=False, stop=True)
                    last.then_inc(S["unit_ready"], 1)

                def weighted(st, off, g, k):
                    if k == 0:
                        if g == 0:
                            pe.wait_ge(S["v_ready"], st.at(off, 1, 1))
                        if not (st.first(off) and g == 0):
                            pe.wait_ge(S["y_kept"], st.at(off, 4, g))
                    pe.wait_ge(S["exp_done"], st.at(off, 20, 5 * g + (2, 4, 5)[k]))
                    for kt in ((0,), (1, 3), (2,))[k]:
                        for hh in range(QUAD):
                            at, col, width = segment(hh, kt)
                            last = pe.matmul(pv[hh * VW:(hh + 1) * VW, kt * P:T],
                                             vaug[st.par(off)][:, kt, g * QUAD + hh, :],
                                             probs[g % 2][:, at * 2 * T + col:at * 2 * T + col + width],
                                             start=kt == 0, stop=kt == 2, skip_group_check=True)
                    if k == 2:
                        last.then_inc(S["pv_ready"], 1)

                def body(st):
                    for g in range(NQUAD):
                        off, pg = (0, g - 1) if g else (-1, NQUAD - 1)
                        for item in plan(g):
                            if item.startswith("unit") and st.has(0):
                                unit(st, g, int(item[4:]))
                            elif item.startswith("pv") and st.has(off):
                                weighted(st, off, pg, int(item[2:]))
                            elif item.startswith("max") and st.has(1):
                                max_bank(st, int(item[3:]))
                            elif item in READERS and st.has(STAGE[item]):
                                job(st, item)

                steps(pe, body)

            @block.scalar
            def _(act):
                def copy(out, in_, done, scale=1.0):
                    act.activation(out, in_, ACT.Copy, scale=scale).then_inc(S[done], 1)

                def job(st, name):
                    if name == "xt":
                        act.wait_ge(S["xT_ps"], st.at(2, 1, 1))
                        if not st.first(2) and (st.every or st.number + 2 >= 2):
                            act.wait_ge(S["v_ps"], st.at(0, 1, 1))
                        copy(xT[st.par(2)][:], misc[:], "xT_ready")
                    elif name in ("q", "k"):
                        w = "qk".index(name)
                        act.wait_ge(S["qk_split"], st.at(2, 4, w + 1))
                        if not st.first(2):
                            act.wait_ge(S["parts_stored"], st.at(1, 16, 16))
                        copy(parts[:, w, 0, :], whole[w][:], "qk_high")
                    elif name in ("qr", "kr"):
                        w = "qk".index(name[0])
                        act.wait_ge(S["qk_split"], st.at(2, 4, w + 3))
                        copy(parts[:, w, 1, :], rest[w][:], "qk_high")
                    elif name == "m":
                        act.wait_ge(S["m_ps"], st.at(1, 1, 1))
                        if not st.first(1):
                            act.wait_ge(S["max_rows"], st.at(0, 48, 48))
                        copy(mparts[:, 0, :], misc[0:NH * QT, 0:P], "m_high", scale=-1.0)
                        act.wait_ge(S["m_rest"], st.at(1, 2, 1))
                        copy(mparts[:, 1, :], mrest[:], "m_high")
                    elif name == "yn":
                        act.wait_ge(S["ynT_ps"], st.at(-1, 1, 1))
                        copy(ynT[:], misc[:], "ynT_ready")
                    elif name == "x1t":
                        act.wait_ge(S["x1T_ps"], st.at(-1, 1, 1))
                        copy(x1T[:], misc[:], "x1T_ready")

                def body(st):
                    for g in range(NQUAD):
                        off, pg = (0, g - 1) if g else (-1, NQUAD - 1)
                        for item in plan(g):
                            if item.startswith("unit") and st.has(0):
                                u = int(item[4:])
                                act.wait_ge(S["unit_ready"], st.at(0, 20, 5 * g + u + 1))
                                if u == 0 and (g >= 2 or not st.first(0)):
                                    act.wait_ge(S["pv_ready"], st.at(0, 4, g - 1))
                                act.activation(probs[g % 2][:, u * 2 * T:(u + 1) * 2 * T],
                                               scores[(5 * g + u) % 2][:], ACT.Exp).then_inc(S["exp_done"], 1)
                            elif item == "pv2" and st.has(off):
                                act.wait_ge(S["pv_ready"], st.at(off, 4, pg + 1))
                                if st.every or st.number + off >= 2:
                                    act.wait_ge(S["y_ps"], st.at(off - 2, 4, 4))
                                copy(yraw[st.par(off)][:, pg, :], pv[:], "y_kept")
                            elif item in STAGE and st.has(STAGE[item]):
                                job(st, item)

                act.wait_ge(S["const_ready"], 9)
                steps(act, body)

            @block.gpsimd
            def _(pool):
                pool.memset(zeros[:], 0.0).then_inc(S["zeros_set"], 1)
                pool.wait_ge(S["const_loaded"], n_const[0])
                pool.memset(minus_half[:], -0.5).then_inc(S["const_ready"], 1)
                pool.memset(eps[:], EPS).then_inc(S["const_ready"], 1)

                def body(st):
                    for g in range(NQUAD):
                        for item in plan(g):
                            if item in ("qr", "kr") and st.has(2):
                                w = "qk".index(item[0])
                                pool.wait_ge(S["qk_high"], st.at(2, 4, w + 3))
                                pool.tensor_tensor(parts[:, w, 2, :], rest[w][:], parts[:, w, 1, :],
                                                   ALU.subtract).then_inc(S["qk_low"], 1)
                            elif item == "o" and st.has(-1):
                                pool.wait_ge(S["ln_done"], st.at(-1, 12, 8))
                                pool.tensor_tensor(var_eps[:].unsqueeze(2), mean_var[:, :, 1:2], eps[:].unsqueeze(2),
                                                   ALU.add).then_inc(S["rstd_ready"], 1)
                                pool.wait_ge(S["rstd_ready"], st.at(-1, 2, 1))
                                pool.tensor_tensor(rstd[:], var_eps[:], minus_half[:],
                                                   ALU.pow).then_inc(S["rstd_ready"], 1)
                            elif item == "x1t" and st.has(-1):
                                pool.wait_ge(S["ln_done"], st.at(-1, 12, 12))
                                pool.tensor_copy(keep["x1"][:, bass.ds((st.number - 1) * QT, QT), :],
                                                 x1_tiles[:]).then_inc(S["x1_kept"], 1)
                            elif item == "y0" and st.has(-1):
                                pool.wait_ge(S["xres_loaded"], st.at(-1, 16, 16))
                                pool.tensor_tensor(xres[:], xres[:], ob[:].unsqueeze(1).to_broadcast([P, QT, C]),
                                                   ALU.add).then_inc(S["res_biased"], 1)

                pool.wait_ge(S["const_ready"], 9)
                steps(pool, body)

            @block.vector
            def _(dve):
                dve.wait_ge(S["const_loaded"], n_const[0])
                dve.tensor_copy(wq[:].rearrange("c (d h) -> c h d", d=HD),
                                wq_in.rearrange("c (h d) -> c h d", d=HD)).then_inc(S["const_ready"], 1)
                dve.tensor_copy(wk[:].rearrange("c (d h) -> c h d", d=HD),
                                wkv_in[:, 0:C].rearrange("c (h d) -> c h d", d=HD)).then_inc(S["const_ready"], 1)
                dve.tensor_scalar(qb_scaled[:], qb[:], SCALE, None, ALU.mult).then_inc(S["const_ready"], 1)
                for n in range(2):
                    dve.memset(vaug[n][:], 0.0).then_inc(S["const_ready"], 1)

                dve.wait_ge(S["const_ready"], 7)
                for n in range(2):
                    dve.memset(vaug[n][:, :, :, HD:HD + 1], 1.0).then_inc(S["const_ready"], 1)
                dve.wait_ge(S["const_ready"], 9)

                def job(st, name):
                    if name in ("q", "k"):
                        w = "qk".index(name)
                        dve.wait_ge(S[name + "_ps"], st.at(2, 1, 1))
                        if not st.first(2):
                            dve.wait_ge(S["qk_split"], st.at(1, 4, w + 3))
                        if w == 0:
                            ins = dve.tensor_scalar(whole[0][:], misc[:], SCALE, qb_scaled[:, 0:1], ALU.mult, ALU.add)
                        else:
                            ins = dve.tensor_scalar(whole[1][:], misc[:], kb[:, 0:1], None, ALU.add)
                        ins.then_inc(S["qk_split"], 1)
                    elif name in ("qr", "kr"):
                        w = "qk".index(name[0])
                        dve.wait_ge(S["qk_high"], st.at(2, 4, w + 1))
                        if not st.first(2):
                            dve.wait_ge(S["qk_low"], st.at(1, 2, w + 1))
                        dve.tensor_tensor(rest[w][:], whole[w][:], parts[:, w, 0, :],
                                          ALU.subtract).then_inc(S["qk_split"], 1)
                    elif name == "v":
                        dve.wait_ge(S["v_ps"], st.at(1, 1, 1))
                        if st.every or st.number + 1 >= 2:
                            dve.wait_ge(S["pv_ready"], st.at(-1, 4, 4))
                        for i in range(QT):
                            ins = dve.tensor_tensor(
                                vaug[st.par(1)][:, i, :, 0:HD],
                                misc[:, i * P:(i + 1) * P].rearrange("p (h d) -> p h d", d=HD),
                                vb[:].rearrange("p (h d) -> p h d", d=HD), ALU.add)
                        ins.then_inc(S["v_ready"], 1)
                    elif name == "m":
                        dve.wait_ge(S["m_high"], st.at(1, 2, 1))
                        if not st.first(1):
                            dve.wait_ge(S["m_high"], st.at(0, 2, 2))
                        dve.scalar_tensor_tensor(mrest[:], misc[0:NH * QT, 0:P], -1.0, mparts[:, 0, :],
                                                 ALU.mult, ALU.subtract).then_inc(S["m_rest"], 1)
                        dve.wait_ge(S["m_high"], st.at(1, 2, 2))
                        dve.wait_ge(S["m_rest"], st.at(1, 2, 1))
                        dve.tensor_tensor(mparts[:, 2, :], mrest[:], mparts[:, 1, :],
                                          ALU.subtract).then_inc(S["m_rest"], 1)
                    elif name[0] == "y" and name[1] != "n":
                        i = int(name[1])
                        dve.wait_ge(S["y_ps"], st.at(-1, 4, i + 1))
                        if i == 0 and not st.first(-1):
                            dve.wait_ge(S["ynT_ps"], st.at(-2, 1, 1))
                        if i or not st.first(-1):
                            dve.wait_ge(S["y_normed"], st.at(-1, 8, 2 * i))
                        view = misc[:].rearrange("p (h c) -> p h c", c=VW)
                        dve.reciprocal(rsum[:].unsqueeze(2), view[:, :, HD:HD + 1]).then_inc(S["y_normed"], 1)
                        dve.wait_ge(S["y_normed"], st.at(-1, 8, 2 * i + 1))
                        dve.tensor_tensor(ynorm[:, i], view[:, :, 0:HD], rsum[:].unsqueeze(2).to_broadcast([P, NH, HD]),
                                          ALU.mult).then_inc(S["y_normed"], 1)
                    elif name == "o":
                        dve.wait_ge(S["o_ps"], st.at(-1, 1, 1))
                        dve.wait_ge(S["res_biased"], st.at(-1, 1, 1))
                        if not st.first(-1):
                            dve.wait_ge(S["ln_done"], st.at(-2, 12, 12))
                            dve.wait_ge(S["x1T_ps"], st.at(-2, 1, 1))
                            dve.wait_ge(S["x1_kept"], st.at(-2, 1, 1))
                        dve.tensor_tensor(x1_tiles[:].rearrange("p i c -> p (i c)"), misc[:],
                                          xres[:].rearrange("p i c -> p (i c)"), ALU.add).then_inc(S["z_ready"], 1)
                        dve.wait_ge(S["z_ready"], st.at(-1, 1, 1))
                        for i in range(QT):
                            dve.bn_stats(stats[:, i, :], x1_tiles[:, i, :]).then_inc(S["ln_done"], 1)
                        dve.wait_ge(S["ln_done"], st.at(-1, 12, 4))
                        dve.sem_inc(S["stats_passed"], 1)
                        for i in range(QT):
                            dve.bn_aggr(mean_var[:, i, :], stats[:, i, :]).then_inc(S["ln_done"], 1)
                        dve.wait_ge(S["rstd_ready"], st.at(-1, 2, 2))
                        for i in range(QT):
                            dve.tensor_scalar(x1_tiles[:, i, :], x1_tiles[:, i, :], mean_var[:, i, 0:1], rstd[:, i:i + 1],
                                              ALU.subtract, ALU.mult).then_inc(S["ln_done"], 1)
                    elif name == "lg":
                        dve.wait_ge(S["lg_ps"], st.at(-1, 1, 1))
                        dve.tensor_copy(keep["logits"][:, bass.ds((st.number - 1) * QT, QT), :],
                                        misc[:, 0:QT * 8].rearrange("p (i e) -> p i e", e=8)).then_inc(S["logits_kept"], 1)

                def take_max(st, n):
                    pair, k = divmod(n, 5)
                    dve.wait_ge(S["max_ready"], st.at(1, MAXB, n + 1))
                    if k == 4:
                        out = maxC[:, 2 * pair:2 * pair + 2, :]
                    else:
                        out = (maxA if k % 2 == 0 else maxB)[:, 2 * pair + k // 2, :].unsqueeze(1)
                    dve.tensor_reduce(out.rearrange("p a b -> p (a b)"), maxed[n % 2][:].rearrange("p (j t) -> p j t", t=P),
                                      AX.X, ALU.max).then_inc(S["max_taken"], 1)
                    if n < MAXB - 1:
                        return
                    dve.wait_ge(S["max_taken"], st.at(1, MAXB, MAXB))
                    if not st.first(1):
                        dve.wait_ge(S["m_ps"], st.at(0, 1, 1))
                    for i, src in ((3, maxA[:]), (2, maxB[:, :, 0:3]), (1, maxC[:])):
                        dve.tensor_reduce(rowmax[:, :, i:i + 1].rearrange("p h i -> p (h i)"), src, AX.X,
                                          ALU.max).then_inc(S["rowmax_ready"], 1)
                    dve.tensor_copy(rowmax[:, :, 0:1], maxB[:, :, 3:4]).then_inc(S["rowmax_ready"], 1)

                def body(st):
                    for g in range(NQUAD):
                        for item in plan(g):
                            if item.startswith("max") and st.has(1):
                                if item == "max0" and not st.first(1):
                                    dve.wait_ge(S["rowmax_ready"], st.at(0, 4, 4))
                                take_max(st, int(item[3:]))
                            elif item in STAGE and st.has(STAGE[item]):
                                job(st, item)

                steps(dve, body)


def routing_constants():
    before = bf16_bits(np.triu(np.ones((P, P), np.float32), 1))
    rank = np.arange(NE, 0, -1, dtype=np.float32)
    slot_row = np.repeat(np.arange(NSLOT, dtype=np.float32) % CSLOT * P, NE - 1).reshape(NSLOT, NE - 1)
    return before, rank, slot_row


SHARED, ROUTED = "shared", "routed"
LEAD = 3


class Segment:

    def __init__(self, kind, first, count, base, mix_chunk, mix_at):
        self.kind, self.first, self.count, self.base = kind, first, count, base
        self.mix_chunk, self.mix_at = mix_chunk, mix_at
        self.steps = range(-LEAD, max(count + 2, mix_at + CT + 1 if mix_chunk is not None else 0))

    def stages(self, n):
        mixing = self.mix_chunk is not None
        return (tuple(0 <= n + off < self.count for off in (3, 1, 0, -1, -2)) + (n - 2 >= TURN,)
                + tuple(mixing and 0 <= n - self.mix_at - off < CT for off in (0, 1))
                + (mixing and n - self.mix_at >= 2,))


SEGMENTS = []
for _kind, _first, _count, _chunk, _at in ((SHARED, 0, CT, None, 0), (ROUTED, 0, CSLOT, None, 0),
                                           (ROUTED, CSLOT, CSLOT, 0, 2), (SHARED, CT, CT, 1, 3)):
    _base = SEGMENTS[-1].base + SEGMENTS[-1].count if SEGMENTS else 0
    SEGMENTS.append(Segment(_kind, _first, _count, _base, _chunk, _at))


class TileStep:

    def __init__(self, seg, number, like):
        self.seg, self.number, self.like = seg, number, like

    def has(self, off):
        return 0 <= self.like + off < self.seg.count

    def ring(self, off, depth):
        return (self.like + off) % depth

    def mixes(self, off):
        return self.seg.mix_chunk is not None and 0 <= self.like - self.seg.mix_at - off < CT

    def token(self, off):
        return self.number - self.seg.mix_at - off

    def token_ring(self, off, depth):
        return (self.like - self.seg.mix_at - off) % depth

    def tile(self, off):
        return self.number + off + self.seg.base


def run_segments(eng, body):
    for seg in SEGMENTS:
        n = seg.steps.start
        while n < seg.steps.stop:
            run = n
            while run < seg.steps.stop and seg.stages(run) == seg.stages(n):
                run += 1
            turns = (run - n) // TURN
            if turns >= 2:
                with eng.Fori(n, n + TURN * turns - (TURN - 1), TURN) as at:
                    for k in range(TURN):
                        body(TileStep(seg, at + k if k else at, n + k))
                n += TURN * turns
            for k in range(n, run):
                body(TileStep(seg, k, k))
            n = run


def experts(nc, io, dram, keep):
    with ExitStack() as ctx:
        def sb(name, shape, dt=F32):
            return ctx.enter_context(nc.sbuf_tensor("e_" + name, shape, dt))

        def ps(name):
            return ctx.enter_context(nc.psum_tensor("e_" + name, [P, T], F32))

        def sem(name):
            return ctx.enter_context(nc.semaphore("e_" + name))

        x1, logits = keep["x1"], keep["logits"]
        ident = sb("ident", [P, P])
        before = sb("before", [P, P], BF16)
        onesb = sb("onesb", [P, P], BF16)
        rank = sb("rank", [P, NE])
        slot_row = sb("slot_row", [1, NSLOT, NE - 1])
        raw_in = [sb("raw_gate", [P, NE + 1, NCH, C]), sb("raw_up", [P, NE + 1, NCH, C])]
        raw_down = sb("raw_down", [P, NE + 1, F])
        w_in = sb("w_in", [P, NE + 1, 2, F])
        w_down = sb("w_down", [P, NE + 1, NCH, C])
        top = [sb("best", [P, NTILE]), sb("second", [P, NTILE])]
        keyed = sb("keyed", [P, NTILE, NE])
        top_key = sb("top_key", [P, NTILE])
        one = [sb("one_best", [P, NTILE, NE]), sb("one_second", [P, NTILE, NE])]
        others = sb("others", [P, NTILE, NE])
        chosen = sb("chosen", [P, NTILE, NE], BF16)
        expo = sb("expo", [P, NTILE, NE])
        ratio = sb("ratio", [P, NTILE])
        norm = sb("norm", [P, NTILE])
        prob = [sb("prob_best", [P, NTILE]), sb("prob_second", [P, NTILE])]
        weight = [sb("weight_best", [P, NTILE]), sb("weight_second", [P, NTILE])]
        counts = sb("counts", [P, GROUPS, CT])
        running = sb("running", [P, GROUPS, CT])
        ones_f = sb("ones_f", [P, GROUPS * CT])
        start = sb("start", [P, GROUPS])
        group_n = sb("group_n", [P, GROUPS])
        group_i = sb("group_i", [P, GROUPS], I32)
        padded = sb("padded", [P, GROUPS])
        ends = sb("ends", [P, GROUPS])
        shift = sb("shift", [P, GROUPS])
        place = sb("place", [P, NTILE, NE])
        place_f = sb("place_f", [P, NTILE])
        place_i = [sb("place_best", [P, NTILE], I32), sb("place_second", [P, NTILE], I32)]
        past = sb("past", [1, NSLOT, NE - 1])
        expert_f = sb("expert_f", [1, NSLOT])
        expert_i = sb("expert_i", [1, NSLOT], I32)
        total = sb("total", [P, NTILE, C])
        xs = sb("xs", [P, TURN, C])
        xT = [sb(f"xT{n}", [P, P]) for n in range(2)]
        gate = [sb(f"gate{n}", [P, F]) for n in range(2)]
        hid = [sb(f"hid{n}", [P, NCH * P]) for n in range(2)]
        hT = [sb(f"hT{n}", [P, NCH * P]) for n in range(2)]
        ys = sb("ys", [P, TURN, C])
        picked = sb("picked", [P, TURN, 2, C])
        mixed = sb("mixed", [P, TURN, C])
        result = sb("result", [P, TURN, C])
        stats = sb("stats", [P, TURN, 6])
        mean_var = sb("mean_var", [P, TURN, 2])
        var_eps = sb("var_eps", [P, TURN])
        minus_half = sb("minus_half", [P, 1])
        rstd = sb("rstd", [P, TURN])

        gate_ps = [ps(f"gate_ps{n}") for n in range(2)]
        up_ps = [ps(f"up_ps{n}") for n in range(2)]
        x_ps, h_ps, y_ps, spare_ps = ps("x_ps"), ps("h_ps"), ps("y_ps"), ps("spare_ps")
        prep_ps = [gate_ps[0], up_ps[0], gate_ps[1], up_ps[1]]

        names = """const_loaded raw_loaded const_set weight_ps weight_kept routed prefix_ps exponents
            x_scattered0 x_scattered1 x_ready xT_kept gate_ready up_ready silu_done hid_done h_ready hT_kept
            y_ready y_taken half_set stats_passed mix_step stats_ready rstd_ready result_ready""".split()
        S = {n: sem(n) for n in names}
        xs_loaded = [sem(f"xs_loaded{n}") for n in range(TURN)]
        y_stored = [[sem(f"y{c}_stored{n}") for n in range(TURN)] for c in range(CHUNKS)]
        picked_in = [sem(f"picked_in{n}") for n in range(TURN)]
        out_stored = [sem(f"out_stored{n}") for n in range(TURN)]
        CONSTS, RAWS, SETS = 16 * 4, 16 * (4 * NCH + 3), 6
        at_routed = {}
        STORED = 16 * (CSLOT // TURN)

        with nc.Block() as block:

            @block.vector
            def _(dve):
                done = [0]

                def link(ins, name=None):
                    done[0] += 1
                    ins.then_inc(S["routed"], 1)
                    dve.wait_ge(S["routed"], done[0])
                    if name:
                        at_routed[name] = done[0]

                dve.memset(onesb[:], 1.0).then_inc(S["const_set"], 1)
                dve.memset(ones_f[:], 1.0).then_inc(S["const_set"], 1)
                for n in range(2):
                    dve.memset(hid[n][:, F:], 0.0).then_inc(S["const_set"], 1)
                dve.wait_ge(S["const_loaded"], CONSTS)
                dve.wait_ge(S["const_set"], 4)
                by_expert = [P, NTILE, NE]

                link(dve.tensor_reduce(top[0][:], logits[:], AX.X, ALU.max))
                for n, src in ((0, logits), (1, others)):
                    link(dve.tensor_tensor(keyed[:], src[:], top[n][:].unsqueeze(2).to_broadcast(by_expert), ALU.is_equal))
                    link(dve.tensor_tensor(keyed[:], keyed[:], rank[:].unsqueeze(1).to_broadcast(by_expert), ALU.mult))
                    link(dve.tensor_reduce(top_key[:], keyed[:], AX.X, ALU.max))
                    link(dve.tensor_tensor(one[n][:], keyed[:], top_key[:].unsqueeze(2).to_broadcast(by_expert), ALU.is_equal))
                    if n == 0:
                        link(dve.scalar_tensor_tensor(others[:], one[0][:], NEG, logits[:], ALU.mult, ALU.add))
                        link(dve.tensor_reduce(top[1][:], others[:], AX.X, ALU.max))
                link(dve.tensor_tensor(chosen[:], one[0][:], one[1][:], ALU.add), "chosen")
                link(dve.tensor_tensor(expo[:], logits[:], top[0][:].unsqueeze(2).to_broadcast(by_expert), ALU.subtract))
                link(dve.tensor_tensor(ratio[:], top[1][:], top[0][:], ALU.subtract), "exponents")

                dve.wait_ge(S["prefix_ps"], 2)
                link(dve.tensor_copy(counts[:].rearrange("p (k e) t -> p k e t", k=CHUNKS),
                                     x_ps[:].rearrange("p (k t e) -> p k e t", k=CHUNKS, e=NE)))
                link(dve.tensor_tensor_scan(running[:].rearrange("p g t -> p (g t)"), ones_f[:],
                                            counts[:].rearrange("p g t -> p (g t)"), 0.0, ALU.mult, ALU.add))
                link(dve.tensor_tensor(start[:], running[:, :, 0], counts[:, :, 0], ALU.subtract))
                link(dve.tensor_tensor(group_n[:], running[:, :, CT - 1], start[:], ALU.subtract))
                link(dve.tensor_scalar(group_i[:], group_n[:], float(P - 1), None, ALU.add))
                tile_bits = P.bit_length() - 1
                link(dve.tensor_scalar(group_i[:], group_i[:], tile_bits, tile_bits,
                                       ALU.logical_shift_right, ALU.logical_shift_left))
                link(dve.tensor_copy(padded[:], group_i[:]))
                for c in range(CHUNKS):
                    g = slice(c * NE, (c + 1) * NE)
                    link(dve.tensor_tensor_scan(ends[:, g], ones_f[:, 0:NE], padded[:, g], 0.0,
                                                ALU.mult, ALU.add))
                link(dve.tensor_tensor(shift[:], ends[:], padded[:], ALU.subtract))
                link(dve.tensor_tensor(shift[:], shift[:], start[:], ALU.subtract))
                link(dve.tensor_tensor(running[:], running[:], counts[:], ALU.subtract))
                link(dve.tensor_tensor(running[:], running[:], shift[:].unsqueeze(2).to_broadcast([P, GROUPS, CT]), ALU.add))
                for c in range(CHUNKS):
                    tiles = slice(c * CT, (c + 1) * CT)
                    link(dve.tensor_tensor(place[:, tiles, :],
                                           spare_ps[:, c * CT * NE:(c + 1) * CT * NE].rearrange("p (t e) -> p t e", e=NE),
                                           running[:, c * NE:(c + 1) * NE, :].rearrange("p e t -> p t e"), ALU.add))
                for n in range(2):
                    link(dve.tensor_tensor(keyed[:], one[n][:], place[:], ALU.mult))
                    link(dve.tensor_reduce(place_f[:], keyed[:], AX.X, ALU.add))
                    link(dve.tensor_copy(place_i[n][:], place_f[:]), "placed")

                for c in range(CHUNKS):
                    s = slice(c * CSLOT, (c + 1) * CSLOT)
                    link(dve.tensor_tensor(past[:, s, :], slot_row[:, s, :],
                                           ends[0:1, c * NE:(c + 1) * NE - 1].unsqueeze(1).to_broadcast([1, CSLOT, NE - 1]),
                                           ALU.is_ge))
                link(dve.tensor_reduce(expert_f[:], past[:], AX.X, ALU.add))
                link(dve.tensor_copy(expert_i[:], expert_f[:]), "experts")

                dve.wait_ge(S["exponents"], 2)
                link(dve.tensor_reduce(norm[:], expo[:], AX.X, ALU.add))
                link(dve.reciprocal(prob[0][:], norm[:]))
                link(dve.tensor_tensor(prob[1][:], ratio[:], prob[0][:], ALU.mult))
                link(dve.tensor_tensor(norm[:], prob[0][:], prob[1][:], ALU.add))
                link(dve.tensor_scalar(norm[:], norm[:], 1e-20, None, ALU.add))
                link(dve.reciprocal(norm[:], norm[:]))
                for n in range(2):
                    link(dve.tensor_tensor(weight[n][:], prob[n][:], norm[:], ALU.mult))

                def body(st):
                    seg = st.seg
                    if st.has(0):
                        k = st.ring(0, 2)
                        dve.wait_ge(S["silu_done"], st.tile(0) + 1)
                        dve.wait_ge(S["up_ready"], st.tile(0) + 1)
                        dve.tensor_tensor(hid[k][:, 0:F], gate[k][:], up_ps[k][:, 0:F], ALU.mult).then_inc(S["hid_done"], 1)
                    if st.has(1):
                        dve.wait_ge(S["x_ready"], st.tile(1) + 1)
                        dve.tensor_copy(xT[st.ring(1, 2)][:], x_ps[:, 0:P]).then_inc(S["xT_kept"], 1)
                    if st.has(-2):
                        dve.wait_ge(S["y_ready"], st.tile(-2) + 1)
                        if seg.kind == SHARED:
                            at = st.number - 2 + seg.first
                            dve.tensor_tensor(total[:, bass.ds(at, 1), :], y_ps[:, 0:C].unsqueeze(1),
                                              x1[:, bass.ds(at, 1), :], ALU.add).then_inc(S["y_taken"], 1)
                        else:
                            chunk, slot = seg.first // CSLOT, st.ring(-2, TURN)
                            if st.like - 2 >= TURN:
                                dve.wait_ge(y_stored[chunk][slot], (st.number - 2 - slot) * (16 // TURN))
                            elif chunk:
                                dve.wait_ge(y_stored[chunk - 1][slot], STORED)
                            dve.tensor_copy(ys[:, slot, :], y_ps[:, 0:C]).then_inc(S["y_taken"], 1)
                    if st.mixes(0):
                        slot, c = st.token_ring(0, TURN), st.token(0)
                        tile = c + seg.mix_chunk * CT
                        shared_before = seg.base if seg.mix_chunk else 0
                        dve.wait_ge(picked_in[slot], (tile - slot) * (32 // TURN) + 32)
                        dve.wait_ge(S["y_taken"], shared_before + c + 1)
                        last = 3 * tile
                        for n in range(2):
                            if n:
                                dve.wait_ge(S["mix_step"], last + 1)
                            dve.scalar_tensor_tensor(mixed[:, slot:slot + 1, :], picked[:, slot, n:n + 1, :],
                                                     weight[n][:, bass.ds(tile, 1)],
                                                     mixed[:, slot:slot + 1, :] if n else total[:, bass.ds(tile, 1), :],
                                                     ALU.mult, ALU.add).then_inc(S["mix_step"], 1)
                        dve.wait_ge(S["mix_step"], last + 2)
                        dve.bn_stats(stats[:, slot, :], mixed[:, slot, :]).then_inc(S["mix_step"], 1)
                        dve.wait_ge(S["mix_step"], last + 3)
                        dve.sem_inc(S["stats_passed"], 1)
                        dve.bn_aggr(mean_var[:, slot, :], stats[:, slot, :]).then_inc(S["stats_ready"], 1)
                    if st.mixes(1):
                        slot, c = st.token_ring(1, TURN), st.token(1)
                        n = c + seg.mix_chunk * CT
                        dve.wait_ge(S["rstd_ready"], 2 * n + 2)
                        if st.like - seg.mix_at - 1 >= TURN or seg.mix_chunk:
                            dve.wait_ge(out_stored[slot], (n - slot) * (16 // TURN))
                        dve.tensor_scalar(result[:, slot, :], mixed[:, slot, :], mean_var[:, slot, 0:1],
                                          rstd[:, slot:slot + 1], ALU.subtract, ALU.mult).then_inc(S["result_ready"], 1)

                run_segments(dve, body)

            @block.sync
            def _(sp):
                for out, in_ in ((ident[:], io["ident"]), (before[:].bitcast(U16), io["before"]),
                                 (rank[:], io["rank"].unsqueeze(0).to_broadcast([P, NE])),
                                 (slot_row[:], io["slot_row"].unsqueeze(0))):
                    sp.dma_start(out, in_).then_inc(S["const_loaded"], 16)
                for raw, name in zip(raw_in, ("gate", "up")):
                    for j, (f0, fw) in enumerate(FCH):
                        sp.dma_start(raw[0:fw, 0:NE, j, :], io["expert_" + name][:, f0:f0 + fw, :]
                                     .rearrange("e p c -> p e c")).then_inc(S["raw_loaded"], 16)
                        sp.dma_start(raw[0:fw, NE, j, :], io["shared_" + name][f0:f0 + fw, :]).then_inc(S["raw_loaded"], 16)
                for e in range(0, NE, NE // 2):
                    sp.dma_start(raw_down[:, e:e + NE // 2, :], io["expert_down"][e:e + NE // 2]
                                 .rearrange("e c f -> c e f")).then_inc(S["raw_loaded"], 16)
                sp.dma_start(raw_down[:, NE, :], io["shared_down"]).then_inc(S["raw_loaded"], 16)

                def body(st):
                    seg = st.seg
                    chunk = seg.first // CSLOT
                    if st.has(3):
                        if seg.kind == ROUTED and st.like == -3:
                            sp.wait_ge(S[f"x_scattered{chunk}"], 32 * CT)
                        slot, n = st.ring(3, TURN), st.number + 3
                        if seg.base or st.like + 3 >= TURN:
                            sp.wait_ge(S["x_ready"], st.tile(3) + 1 - TURN)
                        src = x1[:, bass.ds(n + seg.first, 1), :] if seg.kind == SHARED else \
                            dram["x_sorted"][chunk][bass.ds(n * P, P), :].unsqueeze(1)
                        sp.dma_start(xs[:, slot:slot + 1, :], src).then_inc(xs_loaded[slot], 16)
                    if seg.kind == ROUTED and st.has(-2):
                        slot, n = st.ring(-2, TURN), st.number - 2
                        sp.wait_ge(S["y_taken"], st.tile(-2) + 1)
                        sp.dma_start(dram["y_sorted"][chunk][bass.ds(n * P, P), :], ys[:, slot, :]).then_inc(y_stored[chunk][slot], 16)
                    if st.mixes(1):
                        slot, n = st.token_ring(1, TURN), st.token(1) + seg.mix_chunk * CT
                        sp.wait_ge(S["result_ready"], n + 1)
                        sp.dma_start(dram["out"][bass.ds(n * P, P), :], result[:, slot, :]).then_inc(out_stored[slot], 16)

                run_segments(sp, body)
                for slot in range(TURN):
                    sp.wait_ge(out_stored[slot], 16 * NTILE // TURN)

            @block.tensor
            def _(pe):
                pe.wait_ge(S["const_loaded"], CONSTS)
                pe.wait_ge(S["raw_loaded"], RAWS)
                n = 0
                for e in (NE, *range(NE)):
                    for w in range(3):
                        if n >= len(prep_ps):
                            pe.wait_ge(S["weight_kept"], n - len(prep_ps) + 1)
                        bank = prep_ps[n % len(prep_ps)]
                        for j, (f0, fw) in enumerate(FCH):
                            if w < 2:
                                last = pe.transpose(bank[:, f0:f0 + fw], raw_in[w][0:fw, e, j, :], ident[0:fw, 0:fw])
                            else:
                                last = pe.transpose(bank[0:fw, j * C:(j + 1) * C], raw_down[:, e, f0:f0 + fw], ident[:])
                        last.then_inc(S["weight_ps"], 1)
                        n += 1
                pe.wait_ge(S["const_set"], 4)
                pe.wait_ge(S["routed"], at_routed["chosen"])
                tokens = chosen[:].rearrange("p t e -> p (t e)")
                pe.matmul(spare_ps[:], before[:], tokens, start=True, stop=True).then_inc(S["prefix_ps"], 1)
                pe.matmul(x_ps[:], onesb[:], tokens, start=True, stop=True).then_inc(S["prefix_ps"], 1)
                pe.wait_ge(S["weight_kept"], n)
                pe.wait_ge(S["routed"], at_routed["experts"])

                def expert(st, off):
                    if st.seg.kind == SHARED:
                        return slice(NE, NE + 1)
                    n = st.number + off + st.seg.first
                    return bass.ds(pe.value_load(expert_i[0:1, bass.ds(n, 1)], min_val=0, max_val=NE - 1), 1)

                def body(st):
                    seg = st.seg
                    if st.has(0):
                        k, e = st.ring(0, 2), expert(st, 0)
                        pe.wait_ge(S["xT_kept"], st.tile(0) + 1)
                        if seg.base or st.like >= 2:
                            pe.wait_ge(S["hid_done"], st.tile(0) - 1)
                        pe.matmul(gate_ps[k][:, 0:F], xT[k][:], w_in[:, e, 0, :].rearrange("p a f -> p (a f)"),
                                  start=True, stop=True).then_inc(S["gate_ready"], 1)
                        pe.matmul(up_ps[k][:, 0:F], xT[k][:], w_in[:, e, 1, :].rearrange("p a f -> p (a f)"),
                                  start=True, stop=True).then_inc(S["up_ready"], 1)
                    if st.has(-1):
                        k = st.ring(-1, 2)
                        pe.wait_ge(S["hid_done"], st.tile(-1) + 1)
                        if seg.base or st.like >= 2:
                            pe.wait_ge(S["hT_kept"], st.tile(-1))
                        for j in range(NCH):
                            last = pe.transpose(h_ps[:, j * P:(j + 1) * P], hid[k][:, j * P:(j + 1) * P], ident[:])
                        last.then_inc(S["h_ready"], 1)
                    if st.has(1):
                        if seg.base or st.like >= 0:
                            pe.wait_ge(S["xT_kept"], st.tile(1))
                        slot = st.ring(1, TURN)
                        pe.wait_ge(xs_loaded[slot], (st.tile(1) - slot) * (16 // TURN) + 16)
                        pe.transpose(x_ps[:, 0:P], xs[:, slot, :], ident[:]).then_inc(S["x_ready"], 1)
                    if st.has(-2):
                        k, e = st.ring(-2, 2), expert(st, -2)
                        pe.wait_ge(S["hT_kept"], st.tile(-2) + 1)
                        if seg.base or st.like >= 3:
                            pe.wait_ge(S["y_taken"], st.tile(-2))
                        for j, (f0, fw) in enumerate(FCH):
                            last = pe.matmul(y_ps[:, 0:C], hT[k][0:fw, j * P:(j + 1) * P],
                                             w_down[0:fw, e, j, :].rearrange("p a c -> p (a c)"),
                                             start=j == 0, stop=j == NCH - 1)
                        last.then_inc(S["y_ready"], 1)

                run_segments(pe, body)

            @block.scalar
            def _(act):
                act.wait_ge(S["routed"], at_routed["exponents"])
                for t in (expo[:].rearrange("p t e -> p (t e)"), ratio[:]):
                    act.activation(t, t, ACT.Exp).then_inc(S["exponents"], 1)
                n = 0
                for e in (NE, *range(NE)):
                    for w in range(3):
                        act.wait_ge(S["weight_ps"], n + 1)
                        bank = prep_ps[n % len(prep_ps)]
                        if w < 2:
                            last = act.activation(w_in[:, e, w, :], bank[:, 0:F], ACT.Copy)
                        else:
                            act.activation(w_down[:, e, 0:NCH - 1, :].rearrange("p a c -> p (a c)"),
                                           bank[:, 0:(NCH - 1) * C], ACT.Copy)
                            rows = FCH[-1][1]
                            last = act.activation(w_down[0:rows, e, NCH - 1, :],
                                                  bank[0:rows, (NCH - 1) * C:NCH * C], ACT.Copy)
                        last.then_inc(S["weight_kept"], 1)
                        n += 1

                def body(st):
                    if st.has(0):
                        k = st.ring(0, 2)
                        act.wait_ge(S["gate_ready"], st.tile(0) + 1)
                        act.activation(gate[k][:], gate_ps[k][:, 0:F], ACT.Silu).then_inc(S["silu_done"], 1)
                    if st.has(-1):
                        act.wait_ge(S["h_ready"], st.tile(-1) + 1)
                        act.activation(hT[st.ring(-1, 2)][:], h_ps[:, 0:NCH * P], ACT.Copy).then_inc(S["hT_kept"], 1)

                run_segments(act, body)

            @block.gpsimd
            def _(pool):
                pool.memset(minus_half[:], -0.5).then_inc(S["half_set"], 1)
                pool.wait_ge(S["half_set"], 1)
                pool.wait_ge(S["routed"], at_routed["placed"])
                for c in range(CHUNKS):
                    for t in range(c * CT, (c + 1) * CT):
                        for n in range(2):
                            pool.indirect_dma_start(out=dram["x_sorted"][c],
                                                    out_offset=bass.IndirectOffsetOnAxis(ap=place_i[n][:, t:t + 1], axis=0),
                                                    in_=x1[:, t, :], in_offset=None).then_inc(S[f"x_scattered{c}"], 16)

                def gather(t):
                    for n in range(2):
                        pool.indirect_dma_start(out=picked[:, t % TURN, n, :], out_offset=None, in_=dram["y_sorted"][t // CT],
                                                in_offset=bass.IndirectOffsetOnAxis(ap=place_i[n][:, t:t + 1], axis=0)) \
                            .then_inc(picked_in[t % TURN], 16)

                for c in range(CHUNKS):
                    for slot in range(TURN):
                        pool.wait_ge(y_stored[c][slot], STORED)
                    for t in range(c * CT, c * CT + TURN):
                        gather(t)
                    for t in range(c * CT, (c + 1) * CT):
                        slot = t % TURN
                        pool.wait_ge(S["stats_ready"], t + 1)
                        pool.tensor_scalar(var_eps[:, slot:slot + 1], mean_var[:, slot, 1:2], EPS, None,
                                           ALU.add).then_inc(S["rstd_ready"], 1)
                        pool.wait_ge(S["rstd_ready"], 2 * t + 1)
                        pool.tensor_tensor(rstd[:, slot:slot + 1], var_eps[:, slot:slot + 1], minus_half[:],
                                           ALU.pow).then_inc(S["rstd_ready"], 1)
                        if t + TURN < (c + 1) * CT:
                            gather(t + TURN)


_INPUTS = {"x": "L0_attn_x", "q_w": "L0_attn_q_w", "q_b": "L0_attn_q_b", "kv_w": "L0_attn_kv_w", "kv_b": "L0_attn_kv_b",
           "o_w": "L0_attn_o_w", "o_b": "L0_attn_o_b", "gate_w": "L0_ffn_gate_w", "expert_gate": "L0_ffn_expert_gate",
           "expert_up": "L0_ffn_expert_up", "expert_down": "L0_ffn_expert_down", "shared_gate": "L0_ffn_shared_gate",
           "shared_up": "L0_ffn_shared_up", "shared_down": "L0_ffn_shared_down"}


def constants():
    q, k = stack_constants()
    before, rank, slot_row = routing_constants()
    eye = np.eye(P, dtype=np.float32)
    return {"ident": eye, "identb": bf16_bits(eye), "causal": causal_constants(), "qstack_rows": q,
            "kstack_rows": k, "before": before, "rank": rank, "slot_row": slot_row}


def build(nc, io):
    dram = {"out": io["out"],
            "parts": [nc.dram_tensor(f"parts{n}", (2, PARTS, HD, NH, T), BF16).ap() for n in range(2)],
            "x_sorted": [nc.dram_tensor(f"x_sorted{c}", (CSLOT * P, C), F32).ap() for c in range(CHUNKS)],
            "y_sorted": [nc.dram_tensor(f"y_sorted{c}", (CSLOT * P, C), F32).ap() for c in range(CHUNKS)]}
    with nc.sbuf_tensor("x1_all", [P, NTILE, C], F32) as x1, nc.sbuf_tensor("logits", [P, NTILE, NE], F32) as logits:
        keep = {"x1": x1, "logits": logits}
        attention(nc, io, dram, keep)
        experts(nc, io, dram, keep)


def kernel(**inputs):
    import concourse.bacc as bacc
    from concourse.bass_utils import run_bass_kernel_spmd

    nc = bacc.Bacc("TRN2", target_bir_lowering=False, num_devices=1)
    arrays = {n: np.ascontiguousarray(inputs[source]) for n, source in _INPUTS.items()} | constants()
    io = {n: nc.dram_tensor("in_" + n, a.shape, mybir.dt.from_np(a.dtype), kind="ExternalInput").ap()
          for n, a in arrays.items()}
    io["out"] = nc.dram_tensor("out", (B * T, C), F32, kind="ExternalOutput").ap()
    build(nc, io)
    said = run_bass_kernel_spmd(nc, [{"in_" + n: a for n, a in arrays.items()}], core_ids=[0])
    return np.asarray(said.results[0]["out"]).reshape(B, T, C)
```

```python
from contextlib import ExitStack

import concourse.bass as bass
import numpy as np
from concourse import mybir

F32 = mybir.dt.float32
BF16 = mybir.dt.bfloat16
F32R = mybir.dt.float32r
I32 = mybir.dt.int32
U16 = mybir.dt.uint16
ALU = mybir.AluOpType
ACT = mybir.ActivationFunctionType
AX = mybir.AxisListType

P = 128
B, T, C = 16, 512, 128
NH, HD = 16, 8
QT = T // P
NTILE = B * QT
QUAD = 4
NQUAD = NH // QUAD
UNITS = 10
SB, MB = 2, 4
SEQ_UNITS = NQUAD * UNITS
MAXB = 40
PARTS = 3
PROD = PARTS * PARTS * HD
BIAS_ROWS = 4
CUT = 16
MAX_ROW = 96
STACK_ROWS = 128
VW = 32
SCALE = 1.0 / float(np.sqrt(HD))
NEG = -1.0e38
EPS = 1e-5


def bf16_bits(a):
    return (np.ascontiguousarray(a, np.float32).view(np.uint32) >> np.uint32(16)).astype(np.uint16)


def stack_constants():
    slope = np.arange(1, NH + 1, dtype=np.float32) / NH
    pos = slope[:, None] * np.arange(T, dtype=np.float32)[None, :]
    hi = (pos.view(np.uint32) & np.uint32(0xFFFF0000)).view(np.float32)
    q = np.zeros((STACK_ROWS - PROD, NH, T), np.float32)
    k = np.zeros((STACK_ROWS - PROD, NH, T), np.float32)
    q[0:2] = 1
    k[0], k[1] = hi, pos - hi
    q[2:4] = -k[0:2]
    k[2:4] = 1
    k[MAX_ROW - PROD:MAX_ROW - PROD + PARTS] = 1
    free = [*range(PROD + BIAS_ROWS, MAX_ROW), *range(MAX_ROW + PARTS, STACK_ROWS)]
    block = np.arange(T) // CUT
    for r, row in zip(range(T // CUT - 1), free, strict=False):
        q[row - PROD] = block == r
        k[row - PROD] = np.where(block > r, NEG, 0)
    assert len(free) >= T // CUT - 1
    return bf16_bits(q), bf16_bits(k)


def causal_constant():
    mask = np.triu(np.full((P, P), NEG, np.float32), 1)
    return bf16_bits(mask)


def max_stage(n):
    return 2 if n < 10 else 1


class Step:

    def __init__(self, number, parity, every):
        self.number, self.parity, self.every = number, parity, every

    def has(self, off):
        return self.every or 0 <= self.number + off < B

    def first(self, off):
        return not self.every and self.number + off == 0

    def at(self, off, per_seq, done):
        return (self.number + off) * per_seq + done

    def at_same(self, off, done):
        return (self.number + off - self.par(off)) * (done // 2) + done

    def par(self, off):
        return (self.parity + off) % 2


def segment(hh, kt):
    if kt == 0:
        return hh, 0, T
    if kt == 2:
        return 2 * QUAD + hh // 2, hh % 2 * 2 * P, 2 * P
    return QUAD + hh, 0 if kt == 1 else 3 * P, T - kt * P


KEY_TILES = (0, 1, 3, 2)
NEEDS = (QUAD, 2 * QUAD, 2 * QUAD, UNITS)


MAX_AT = (10, 20, 30, 0)
JOBS = (("xt", "q", "k", "qr", "kr"), ("y0", "y1", "y2", "y3", "v"), ("yn", "o", "ln", "x1t"), ("m", "mr", "lg"))


def plan(g):
    score = "unit0 unit1 pv0 unit2 unit3 unit4 pv1 unit5 unit6 pv2 unit7 pv3 unit8 unit9".split()
    maxes = [f"max{MAX_AT[g] + n}" for n in range(10)]
    jobs = list(JOBS[g])
    keyed = []
    for rank, items in enumerate((score, jobs, maxes)):
        lead = 0.5 if rank < 2 else 0.05
        keyed += [((n + lead) / len(items), rank, n, x) for n, x in enumerate(items)]
    if g == 3:
        early = {"m": 0.08, "mr": 0.25}
        keyed = [(early.get(x, a), r, n, x) for a, r, n, x in keyed]
    return [x for *_, x in sorted(keyed)]


READERS = {
    "xt": ("xT_ready", 1, 1), "q": ("qk_split", 4, 1), "k": ("qk_split", 4, 2),
    "y0": ("y_normed", 8, 2), "y1": ("y_normed", 8, 4), "y2": ("y_normed", 8, 6), "y3": ("y_normed", 8, 8),
    "v": ("v_ready", 1, 1), "yn": ("ynT_ready", 1, 1), "o": ("z_ready", 1, 1), "x1t": ("x1T_ready", 1, 1),
    "m": ("m_rest", 2, 1), "lg": ("logits_kept", 1, 1),
}
STAGE = {"xt": 2, "q": 2, "k": 2, "qr": 2, "kr": 2, "v": 1, "m": 1, "mr": 1, "yn": -1, "o": -1, "ln": -1, "x1t": -1, "lg": -1,
         "y0": -1, "y1": -1, "y2": -1, "y3": -1}
BANK_ORDER = [j for g in range(NQUAD) for j in plan(g) if j in READERS]


def bank_before(st, job):
    n = BANK_ORDER.index(job)
    for back in range(0, 3):
        order = BANK_ORDER[:n] if back == 0 else BANK_ORDER
        for j in reversed(order):
            if st.every or 0 <= st.number - back + STAGE[j] < B:
                return j, STAGE[j] - back
    return None


NE = 8
F = 352
FCH = [(j, min(P, F - j)) for j in range(0, F, P)]
NCH = len(FCH)
TURN = 4
CHUNKS = 2
CT = NTILE // CHUNKS
GROUPS = CHUNKS * NE
CSLOT = -(-(2 * CT + NE - 1) // TURN) * TURN
NSLOT = CHUNKS * CSLOT


def attention(nc, io, dram, keep):
    with ExitStack() as ctx:
        def sb(name, shape, dt=F32):
            return ctx.enter_context(nc.sbuf_tensor(name, shape, dt))

        def ps(name, cols=T):
            return ctx.enter_context(nc.psum_tensor(name, [P, cols], F32))

        def sem(name):
            return ctx.enter_context(nc.semaphore(name))

        ident = sb("ident", [P, P])
        identb = sb("identb", [P, P], BF16)
        causal = sb("causal", [P, P], BF16)
        zeros = sb("zeros", [P, C])
        wkv_in = sb("wkv_in", [P, 2 * C])
        wq = sb("wq", [P, C])
        wk = sb("wk", [P, C])
        wo = sb("wo", [P, C])
        qb = sb("qb", [P, 1])
        qb_scaled = sb("qb_scaled", [P, 1])
        kb = sb("kb", [P, 1])
        vb = sb("vb", [P, C])
        ob = sb("ob", [P, C])
        gw = sb("gw", [P, 8])
        xin = [sb(f"xin{n}", [P, QT, C]) for n in range(2)]
        xT = [sb(f"xT{n}", [P, T]) for n in range(2)]
        qstack = [sb(f"qstack{n}", [P, NH, T], BF16) for n in range(2)]
        kstack = [sb(f"kstack{n}", [P, NH, T], BF16) for n in range(2)]
        vaug = [sb(f"vaug{n}", [P, QT, NH, VW]) for n in range(2)]
        yraw = [sb(f"yraw{n}", [P, NQUAD, T]) for n in range(2)]
        probs = [sb(f"probs{n}", [P, UNITS * T]) for n in range(2)]
        whole = [sb(n, [P, T]) for n in ("q_whole", "k_whole")]
        rest = [sb(n, [P, T]) for n in ("q_rest", "k_rest")]
        wq_in = rest[0][:, 0:C]
        parts = sb("parts", [P, 2, PARTS, T], BF16)
        maxA = sb("maxA", [P, NH, 4])
        maxB = sb("maxB", [P, NH, 4])
        maxC = sb("maxC", [P, NH, 2])
        rowmax = sb("rowmax", [P, NH, QT])
        mparts = sb("mparts", [NH * QT, PARTS, P], BF16)
        mrest = sb("mrest", [NH * QT, P])
        rsum = sb("rsum", [P, NH])
        ynorm = sb("ynorm", [P, QT, NH, HD])
        ynT = sb("ynT", [P, T])
        xres = sb("xres", [P, QT, C])
        stats = sb("stats", [P, QT, 6])
        mean_var = sb("mean_var", [P, QT, 2])
        rstd = sb("rstd", [P, QT])
        var_eps = sb("var_eps", [P, QT])
        minus_half = sb("minus_half", [P, QT])
        eps = sb("eps", [P, QT])
        x1_tiles = sb("x1_tiles", [P, QT, C])
        x1T = ynT

        scores = [ps(f"scores{n}") for n in range(SB)]
        maxed = [ps(f"maxed{n}") for n in range(MB)]
        pv = ps("pv")
        misc = ps("misc")

        names = """const_loaded stack_rows_loaded const_ready unit_ready max_ready pv_ready xT_ps q_ps k_ps v_ps m_ps y_ps ynT_ps o_ps
            x1T_ps lg_ps exp_done xT_ready qk_high y_kept m_high ynT_ready x1T_ready max_taken rowmax_ready
            qk_split m_rest v_ready y_normed z_ready ln_done rstd_ready logits_kept zeros_set rows_zeroed masked qk_low res_biased x1_kept x_loaded0 x_loaded1 stats_passed maxima_passed exp_passed
            xres_loaded parts_stored max_rows""".split()
        S = {n: sem(n) for n in names}
        n_const = [0]
        x_loaded = [S["x_loaded0"], S["x_loaded1"]]
        stack_loaded = [[sem(f"stack{n}_loaded{g}") for g in range(NQUAD)] for n in range(2)]

        def ready(eng, st, job):
            before = bank_before(st, job)
            if before:
                name, per, done = READERS[before[0]]
                eng.wait_ge(S[name], st.at(before[1], per, done))

        def steps(eng, body):
            for n in range(-3, 3):
                body(Step(n, n % 2, False))
            with eng.Fori(3, B - 4, 2) as n:
                body(Step(n, 1, True))
                body(Step(n + 1, 0, True))
            for n in (B - 3, B - 2, B - 1, B):
                body(Step(n, n % 2, False))

        with nc.Block() as block:

            @block.sync
            def _(sp):
                sp.wait_ge(S["zeros_set"], 1)

                def const(out, in_):
                    sp.dma_start(out, in_).then_inc(S["const_loaded"], 16)
                    n_const[0] += 16

                const(ident[:], io["ident"])
                const(identb[:].bitcast(U16), io["identb"])
                const(causal[:].bitcast(U16), io["causal"])
                const(wq_in, io["q_w"])
                const(wkv_in[:], io["kv_w"])
                const(wo[:], io["o_w"])
                const(vb[:], io["kv_b"][C:2 * C].unsqueeze(0).to_broadcast([P, C]))
                const(ob[:], io["o_b"].unsqueeze(0).to_broadcast([P, C]))
                with nc.allow_non_contiguous_dma(reason="biases by (width, head), and the router's weights transposed"):
                    const(qb[:], io["q_b"].rearrange("(h d u) -> d h u", d=HD, u=1))
                    const(kb[:], io["kv_b"][0:C].rearrange("(h d u) -> d h u", d=HD, u=1))
                    const(gw[:], io["gate_w"].rearrange("e c -> c e"))
                const(keep["rank"][:], io["rank"].unsqueeze(0).to_broadcast([P, NE]))

                def load_stack(st, g):
                    src = dram["parts"][st.par(2)]
                    heads = slice(g * QUAD, (g + 1) * QUAD)
                    to_q, to_k = qstack[st.par(2)], kstack[st.par(2)]
                    rows = PARTS * HD
                    for a in range(PARTS):
                        sp.dma_start(to_q[a * rows:(a + 1) * rows, heads, :],
                                     src[0, a, :, heads, :].unsqueeze(0).to_broadcast([PARTS, HD, QUAD, T])
                                     .rearrange("c d h t -> c d (h t)")).then_inc(stack_loaded[st.par(2)][g], 16)
                    sp.dma_start(to_k[0:PROD, heads, :],
                                 src[1, :, :, heads, :].rearrange("a d h t -> (a d) (h t)").unsqueeze(0)
                                 .to_broadcast([PARTS, rows, QUAD * T])).then_inc(stack_loaded[st.par(2)][g], 16)

                def body(st):
                    if st.has(3):
                        if not st.first(3) and (st.every or st.number + 3 >= 2):
                            sp.wait_ge(S["xT_ps"], st.at(1, 1, 1))
                        sp.dma_start(xin[st.par(3)][:], io["x"][bass.ds(st.number + 3, 1)]
                                     .rearrange("b (i p) c -> p (b i) c", p=P)).then_inc(x_loaded[st.par(3)], 16)
                    if st.has(-1):
                        if not st.first(-1):
                            sp.wait_ge(S["z_ready"], st.at(-2, 1, 1))
                        sp.dma_start(xres[:], io["x"][bass.ds(st.number - 1, 1)]
                                     .rearrange("b (i p) c -> p (b i) c", p=P)).then_inc(S["xres_loaded"], 16)
                    if st.has(2):
                        sp.wait_ge(S["qk_low"], st.at(2, 2, 2))
                        sp.wait_ge(S["qk_high"], st.at(2, 4, 4))
                        sp.dma_start(dram["parts"][st.par(2)].rearrange("w a d h t -> (d h) (w a) t"),
                                     parts[:].rearrange("p w a t -> p (w a) t")).then_inc(S["parts_stored"], 16)
                        sp.wait_ge(S["parts_stored"], st.at(2, 16, 16))
                    if st.has(0):
                        rows, part = CSLOT * P // B, P // 2
                        for sorted_rows in dram["x_sorted"]:
                            sp.dma_start(sorted_rows[bass.ds(st.number * rows, rows), :]
                                         .rearrange("(n p) c -> p n c", p=part),
                                         zeros[0:part, :].unsqueeze(1).to_broadcast([part, rows // part, C])) \
                                .then_inc(S["rows_zeroed"], 16)
                    for g in range(NQUAD):
                        if g == 3 and st.has(1):
                            sp.wait_ge(S["m_rest"], st.at(1, 2, 2))
                            sp.wait_ge(S["m_high"], st.at(1, 2, 2))
                            for a in range(PARTS):
                                sp.dma_start(qstack[st.par(1)][MAX_ROW + a:MAX_ROW + a + 1, :, :]
                                             .rearrange("a h (i t) -> a (h i) t", t=P),
                                             mparts[:, a, :]).then_inc(S["max_rows"], 16)
                        if st.has(2):
                            if st.has(0):
                                sp.wait_ge(S["unit_ready"], st.at(0, SEQ_UNITS, UNITS * (g + 1)))
                            load_stack(st, g)

                steps(sp, body)
                sp.wait_ge(S["rows_zeroed"], 16 * B * CHUNKS)

            @block.tensor
            def _(pe):
                pe.wait_ge(S["const_loaded"], n_const[0])
                pe.wait_ge(S["const_ready"], 9)

                def transposes(srcs, done):
                    for n, src in enumerate(srcs):
                        last = pe.transpose(misc[0:src.shape[1], n * P:(n + 1) * P], src, ident[:])
                    last.then_inc(S[done], 1)

                def job(st, name):
                    ready(pe, st, name)
                    if name == "xt":
                        pe.wait_ge(x_loaded[st.par(2)], st.at_same(2, 16))
                        transposes([xin[st.par(2)][:, i, :] for i in range(QT)], "xT_ps")
                    elif name in ("q", "k"):
                        pe.wait_ge(S["xT_ready"], st.at(2, 1, 1))
                        w = wq if name == "q" else wk
                        pe.matmul(misc[:], w[:], xT[st.par(2)][:], start=True, stop=True).then_inc(S[name + "_ps"], 1)
                    elif name == "v":
                        for i in range(QT):
                            last = pe.matmul(misc[:, i * P:(i + 1) * P], xT[st.par(1)][:, i * P:(i + 1) * P],
                                             wkv_in[:, C:2 * C], start=True, stop=True)
                        last.then_inc(S["v_ps"], 1)
                    elif name == "m":
                        pe.wait_ge(S["rowmax_ready"], st.at(1, 4, 4))
                        pe.sem_inc(S["maxima_passed"], 1)
                        transposes([rowmax[:].rearrange("p h i -> p (h i)")], "m_ps")
                    elif name[0] == "y" and name[1] != "n":
                        i = int(name[1])
                        if i == 0:
                            pe.wait_ge(S["y_kept"], st.at(-1, 4, 4))
                        transposes([yraw[st.par(-1)][:, g, i * P:(i + 1) * P] for g in range(NQUAD)], "y_ps")
                    elif name == "yn":
                        pe.wait_ge(S["y_normed"], st.at(-1, 8, 8))
                        transposes([ynorm[:, i].rearrange("p h d -> p (h d)") for i in range(QT)], "ynT_ps")
                    elif name == "o":
                        pe.wait_ge(S["ynT_ready"], st.at(-1, 1, 1))
                        for i in range(QT):
                            last = pe.matmul(misc[:, i * P:(i + 1) * P], ynT[:, i * P:(i + 1) * P], wo[:],
                                             start=True, stop=True)
                        last.then_inc(S["o_ps"], 1)
                    elif name == "x1t":
                        pe.wait_ge(S["ln_done"], st.at(-1, 12, 12))
                        transposes([x1_tiles[:, i, :] for i in range(QT)], "x1T_ps")
                    elif name == "lg":
                        pe.wait_ge(S["x1T_ready"], st.at(-1, 1, 1))
                        for i in range(QT):
                            last = pe.matmul(misc[:, i * 8:(i + 1) * 8], x1T[:, i * P:(i + 1) * P], gw[:],
                                             start=True, stop=True)
                        last.then_inc(S["lg_ps"], 1)

                def max_bank(st, n):
                    pair, k = divmod(n, 5)
                    off = max_stage(n)
                    if n == 0 and st.first(off):
                        pe.wait_ge(S["stack_rows_loaded"], 64)
                    if k in (0, 2, 4):
                        head = 2 * pair + (k == 2) + (k == 4)
                        if k != 2 or head % QUAD == 0:
                            pe.wait_ge(stack_loaded[st.par(off)][head // QUAD], st.at_same(off, 64))
                    if n >= MB or not st.first(off):
                        pe.wait_ge(S["max_taken"], st.at(off, MAXB, n - MB + 1))
                    bank = maxed[n % MB]
                    q, ks = qstack[st.par(off)], kstack[st.par(off)]
                    if k == 4:
                        blocks = [(2 * pair, 1, 0), (2 * pair + 1, 1, 2 * P)]
                    elif k % 2 == 0:
                        blocks = [(2 * pair + k // 2, 3, 0)]
                    else:
                        blocks = [(2 * pair + k // 2, 2, 0), (2 * pair + k // 2, 0, 3 * P)]
                    for h, i, col in blocks:
                        pe.matmul(bank[:, col:col + (i + 1) * P], q[0:MAX_ROW, h, i * P:(i + 1) * P],
                                  ks[0:MAX_ROW, h, 0:(i + 1) * P], start=True, stop=False)
                        last = pe.matmul(bank[:, col + i * P:col + (i + 1) * P], identb[:], causal[:],
                                         start=False, stop=True)
                    last.then_inc(S["max_ready"], 1)

                def unit(st, g, u):
                    n = UNITS * g + u
                    if n == 0:
                        pe.wait_ge(S["max_rows"], st.at(0, 48, 48))
                    if n >= SB or not st.first(0):
                        pe.wait_ge(S["exp_done"], st.at(0, SEQ_UNITS, n - SB + 1))
                    for hh in range(QUAD):
                        for kt in range(QT):
                            at, col, width = segment(hh, kt)
                            if at == u:
                                h = g * QUAD + hh
                                last = pe.matmul(scores[n % SB][:, col:col + width],
                                                 kstack[st.par(0)][:, h, kt * P:(kt + 1) * P],
                                                 qstack[st.par(0)][:, h, kt * P:T], start=True, stop=True)
                    last.then_inc(S["unit_ready"], 1)

                def weighted(st, off, g, k):
                    if k == 0:
                        if g == 0:
                            pe.wait_ge(S["v_ready"], st.at(off, 1, 1))
                        if not (st.first(off) and g == 0):
                            pe.wait_ge(S["y_kept"], st.at(off, 4, g))
                    pe.wait_ge(S["masked"], st.at(off, SEQ_UNITS, UNITS * g + NEEDS[k]))
                    kt = KEY_TILES[k]
                    for hh in range(QUAD):
                        at, col, width = segment(hh, kt)
                        last = pe.matmul(pv[hh * VW:(hh + 1) * VW, kt * P:T], vaug[st.par(off)][:, kt, g * QUAD + hh, :],
                                         probs[g % 2][:, at * T + col:at * T + col + width],
                                         start=k == 0, stop=k == QT - 1, skip_group_check=True)
                    if k == QT - 1:
                        last.then_inc(S["pv_ready"], 1)

                def body(st):
                    for g in range(NQUAD):
                        off, pg = (0, g - 1) if g else (-1, NQUAD - 1)
                        for item in plan(g):
                            if item.startswith("unit") and st.has(0):
                                unit(st, g, int(item[4:]))
                            elif item.startswith("pv") and st.has(off):
                                weighted(st, off, pg, int(item[2:]))
                            elif item.startswith("max") and st.has(max_stage(int(item[3:]))):
                                max_bank(st, int(item[3:]))
                            elif item in READERS and st.has(STAGE[item]):
                                job(st, item)

                steps(pe, body)

            @block.scalar
            def _(act):
                def copy(out, in_, done, scale=1.0):
                    act.activation(out, in_, ACT.Copy, scale=scale).then_inc(S[done], 1)

                def job(st, name):
                    if name == "xt":
                        act.wait_ge(S["xT_ps"], st.at(2, 1, 1))
                        if not st.first(2) and (st.every or st.number + 2 >= 2):
                            act.wait_ge(S["v_ps"], st.at(0, 1, 1))
                        copy(xT[st.par(2)][:], misc[:], "xT_ready")
                    elif name in ("q", "k"):
                        w = "qk".index(name)
                        act.wait_ge(S["qk_split"], st.at(2, 4, w + 1))
                        if not st.first(2):
                            act.wait_ge(S["parts_stored"], st.at(1, 16, 16))
                        copy(parts[:, w, 0, :], whole[w][:], "qk_high")
                    elif name in ("qr", "kr"):
                        w = "qk".index(name[0])
                        act.wait_ge(S["qk_split"], st.at(2, 4, w + 3))
                        copy(parts[:, w, 1, :], rest[w][:], "qk_high")
                    elif name == "m":
                        act.wait_ge(S["m_ps"], st.at(1, 1, 1))
                        if not st.first(1):
                            act.wait_ge(S["max_rows"], st.at(0, 48, 48))
                        copy(mparts[:, 0, :], misc[0:NH * QT, 0:P], "m_high", scale=-1.0)
                    elif name == "mr":
                        act.wait_ge(S["m_rest"], st.at(1, 2, 1))
                        copy(mparts[:, 1, :], mrest[:], "m_high")
                    elif name == "yn":
                        act.wait_ge(S["ynT_ps"], st.at(-1, 1, 1))
                        copy(ynT[:], misc[:], "ynT_ready")
                    elif name == "x1t":
                        act.wait_ge(S["x1T_ps"], st.at(-1, 1, 1))
                        copy(x1T[:], misc[:], "x1T_ready")

                def body(st):
                    for g in range(NQUAD):
                        off, pg = (0, g - 1) if g else (-1, NQUAD - 1)
                        for item in plan(g):
                            if item.startswith("unit") and st.has(0):
                                u = int(item[4:])
                                act.wait_ge(S["unit_ready"], st.at(0, SEQ_UNITS, UNITS * g + u + 1))
                                if u == 0 and (g >= 2 or not st.first(0)):
                                    act.wait_ge(S["pv_ready"], st.at(0, 4, g - 1))
                                act.activation(probs[g % 2][:, u * T:(u + 1) * T],
                                               scores[(UNITS * g + u) % SB][:], ACT.Exp).then_inc(S["exp_done"], 1)
                            elif item == "pv3" and st.has(off):
                                act.wait_ge(S["pv_ready"], st.at(off, 4, pg + 1))
                                if st.every or st.number + off >= 2:
                                    act.wait_ge(S["y_ps"], st.at(off - 2, 4, 4))
                                copy(yraw[st.par(off)][:, pg, :], pv[:], "y_kept")
                            elif item in STAGE and st.has(STAGE[item]):
                                job(st, item)

                for n in range(2):
                    act.dma_start(qstack[n][PROD:, :, :].bitcast(U16), io["qstack_rows"]).then_inc(S["stack_rows_loaded"], 16)
                    act.dma_start(kstack[n][PROD:, :, :].bitcast(U16), io["kstack_rows"]).then_inc(S["stack_rows_loaded"], 16)
                act.wait_ge(S["const_ready"], 9)
                steps(act, body)

            @block.gpsimd
            def _(pool):
                pool.memset(zeros[:], 0.0).then_inc(S["zeros_set"], 1)
                pool.wait_ge(S["const_loaded"], n_const[0])
                pool.memset(minus_half[:], -0.5).then_inc(S["const_ready"], 1)
                pool.memset(eps[:], EPS).then_inc(S["const_ready"], 1)

                def body(st):
                    for g in range(NQUAD):
                        for item in plan(g):
                            if item.startswith("unit") and st.has(0):
                                u = int(item[4:])
                                at = probs[g % 2][:, u * T:(u + 1) * T].rearrange("p (i t) -> p i t", t=P)
                                view = at[:, 0, :] if u < QUAD else at[:, 0:QT:QT - 1, :] if u < 2 * QUAD else at[:, 0:QT:2, :]
                                pattern = [[1, P]] if u < QUAD else [[0, 2], [1, P]]
                                pool.wait_ge(S["exp_done"], st.at(0, SEQ_UNITS, UNITS * g + u + 1))
                                pool.sem_inc(S["exp_passed"], 1)
                                pool.affine_select(out=view, in_=view, compare_op=ALU.is_ge, fill=0.0, base=0,
                                                   pattern=pattern, channel_multiplier=-1).then_inc(S["masked"], 1)
                            elif item in ("qr", "kr") and st.has(2):
                                w = "qk".index(item[0])
                                pool.wait_ge(S["qk_high"], st.at(2, 4, w + 3))
                                pool.tensor_tensor(parts[:, w, 2, :], rest[w][:], parts[:, w, 1, :],
                                                   ALU.subtract).then_inc(S["qk_low"], 1)
                            elif item == "o" and st.has(-1):
                                pool.wait_ge(S["ln_done"], st.at(-1, 12, 8))
                                pool.tensor_tensor(var_eps[:].unsqueeze(2), mean_var[:, :, 1:2], eps[:].unsqueeze(2),
                                                   ALU.add).then_inc(S["rstd_ready"], 1)
                                pool.wait_ge(S["rstd_ready"], st.at(-1, 2, 1))
                                pool.tensor_tensor(rstd[:], var_eps[:], minus_half[:],
                                                   ALU.pow).then_inc(S["rstd_ready"], 1)
                            elif item == "x1t" and st.has(-1):
                                pool.wait_ge(S["ln_done"], st.at(-1, 12, 12))
                                pool.tensor_copy(keep["x1"][:, bass.ds((st.number - 1) * QT, QT), :],
                                                 x1_tiles[:]).then_inc(S["x1_kept"], 1)
                            elif item == "y0" and st.has(-1):
                                pool.wait_ge(S["xres_loaded"], st.at(-1, 16, 16))
                                pool.tensor_tensor(xres[:], xres[:], ob[:].unsqueeze(1).to_broadcast([P, QT, C]),
                                                   ALU.add).then_inc(S["res_biased"], 1)

                pool.wait_ge(S["const_ready"], 9)
                steps(pool, body)

            @block.vector
            def _(dve):
                dve.wait_ge(S["const_loaded"], n_const[0])
                dve.tensor_copy(wq[:].rearrange("c (d h) -> c h d", d=HD),
                                wq_in.rearrange("c (h d) -> c h d", d=HD)).then_inc(S["const_ready"], 1)
                dve.tensor_copy(wk[:].rearrange("c (d h) -> c h d", d=HD),
                                wkv_in[:, 0:C].rearrange("c (h d) -> c h d", d=HD)).then_inc(S["const_ready"], 1)
                dve.tensor_scalar(qb_scaled[:], qb[:], SCALE, None, ALU.mult).then_inc(S["const_ready"], 1)
                for n in range(2):
                    dve.memset(vaug[n][:], 0.0).then_inc(S["const_ready"], 1)

                dve.wait_ge(S["const_ready"], 7)
                for n in range(2):
                    dve.memset(vaug[n][:, :, :, HD:HD + 1], 1.0).then_inc(S["const_ready"], 1)
                dve.wait_ge(S["const_ready"], 9)

                def job(st, name):
                    if name in ("q", "k"):
                        w = "qk".index(name)
                        dve.wait_ge(S[name + "_ps"], st.at(2, 1, 1))
                        if not st.first(2):
                            dve.wait_ge(S["qk_split"], st.at(1, 4, w + 3))
                        if w == 0:
                            ins = dve.tensor_scalar(whole[0][:], misc[:], SCALE, qb_scaled[:, 0:1], ALU.mult, ALU.add)
                        else:
                            ins = dve.tensor_scalar(whole[1][:], misc[:], kb[:, 0:1], None, ALU.add)
                        ins.then_inc(S["qk_split"], 1)
                    elif name in ("qr", "kr"):
                        w = "qk".index(name[0])
                        dve.wait_ge(S["qk_high"], st.at(2, 4, w + 1))
                        if not st.first(2):
                            dve.wait_ge(S["qk_low"], st.at(1, 2, w + 1))
                        dve.tensor_tensor(rest[w][:], whole[w][:], parts[:, w, 0, :],
                                          ALU.subtract).then_inc(S["qk_split"], 1)
                    elif name == "v":
                        dve.wait_ge(S["v_ps"], st.at(1, 1, 1))
                        if st.every or st.number + 1 >= 2:
                            dve.wait_ge(S["pv_ready"], st.at(-1, 4, 4))
                        for i in range(QT):
                            ins = dve.tensor_tensor(
                                vaug[st.par(1)][:, i, :, 0:HD],
                                misc[:, i * P:(i + 1) * P].rearrange("p (h d) -> p h d", d=HD),
                                vb[:].rearrange("p (h d) -> p h d", d=HD), ALU.add)
                        ins.then_inc(S["v_ready"], 1)
                    elif name == "m":
                        dve.wait_ge(S["m_high"], st.at(1, 2, 1))
                        if not st.first(1):
                            dve.wait_ge(S["m_high"], st.at(0, 2, 2))
                        dve.scalar_tensor_tensor(mrest[:], misc[0:NH * QT, 0:P], -1.0, mparts[:, 0, :],
                                                 ALU.mult, ALU.subtract).then_inc(S["m_rest"], 1)
                    elif name == "mr":
                        dve.wait_ge(S["m_high"], st.at(1, 2, 2))
                        dve.wait_ge(S["m_rest"], st.at(1, 2, 1))
                        dve.tensor_tensor(mparts[:, 2, :], mrest[:], mparts[:, 1, :],
                                          ALU.subtract).then_inc(S["m_rest"], 1)
                    elif name[0] == "y" and name[1] != "n":
                        i = int(name[1])
                        dve.wait_ge(S["y_ps"], st.at(-1, 4, i + 1))
                        if i == 0 and not st.first(-1):
                            dve.wait_ge(S["ynT_ps"], st.at(-2, 1, 1))
                        if i or not st.first(-1):
                            dve.wait_ge(S["y_normed"], st.at(-1, 8, 2 * i))
                        view = misc[:].rearrange("p (h c) -> p h c", c=VW)
                        dve.reciprocal(rsum[:].unsqueeze(2), view[:, :, HD:HD + 1]).then_inc(S["y_normed"], 1)
                        dve.wait_ge(S["y_normed"], st.at(-1, 8, 2 * i + 1))
                        dve.tensor_tensor(ynorm[:, i], view[:, :, 0:HD], rsum[:].unsqueeze(2).to_broadcast([P, NH, HD]),
                                          ALU.mult).then_inc(S["y_normed"], 1)
                    elif name == "o":
                        dve.wait_ge(S["o_ps"], st.at(-1, 1, 1))
                        dve.wait_ge(S["res_biased"], st.at(-1, 1, 1))
                        if not st.first(-1):
                            dve.wait_ge(S["ln_done"], st.at(-2, 12, 12))
                            dve.wait_ge(S["x1T_ps"], st.at(-2, 1, 1))
                            dve.wait_ge(S["x1_kept"], st.at(-2, 1, 1))
                        dve.tensor_tensor(x1_tiles[:].rearrange("p i c -> p (i c)"), misc[:],
                                          xres[:].rearrange("p i c -> p (i c)"), ALU.add).then_inc(S["z_ready"], 1)
                        dve.wait_ge(S["z_ready"], st.at(-1, 1, 1))
                        for i in range(QT):
                            dve.bn_stats(stats[:, i, :], x1_tiles[:, i, :]).then_inc(S["ln_done"], 1)
                        dve.wait_ge(S["ln_done"], st.at(-1, 12, 4))
                        dve.sem_inc(S["stats_passed"], 1)
                        for i in range(QT):
                            dve.bn_aggr(mean_var[:, i, :], stats[:, i, :]).then_inc(S["ln_done"], 1)
                    elif name == "ln":
                        dve.wait_ge(S["rstd_ready"], st.at(-1, 2, 2))
                        for i in range(QT):
                            dve.tensor_scalar(x1_tiles[:, i, :], x1_tiles[:, i, :], mean_var[:, i, 0:1], rstd[:, i:i + 1],
                                              ALU.subtract, ALU.mult).then_inc(S["ln_done"], 1)
                    elif name == "lg":
                        dve.wait_ge(S["lg_ps"], st.at(-1, 1, 1))
                        dve.tensor_copy(keep["logits"][:, bass.ds((st.number - 1) * QT, QT), :],
                                        misc[:, 0:QT * 8].rearrange("p (i e) -> p i e", e=8)).then_inc(S["logits_kept"], 1)

                def take_max(st, n):
                    pair, k = divmod(n, 5)
                    dve.wait_ge(S["max_ready"], st.at(max_stage(n), MAXB, n + 1))
                    if k == 4:
                        out = maxC[:, 2 * pair:2 * pair + 2, :]
                    else:
                        out = (maxA if k % 2 == 0 else maxB)[:, 2 * pair + k // 2, :].unsqueeze(1)
                    dve.tensor_reduce(out.rearrange("p a b -> p (a b)"), maxed[n % MB][:].rearrange("p (j t) -> p j t", t=P),
                                      AX.X, ALU.max).then_inc(S["max_taken"], 1)
                    if n < MAXB - 1:
                        return
                    dve.wait_ge(S["max_taken"], st.at(1, MAXB, MAXB))
                    if not st.first(1):
                        dve.wait_ge(S["m_ps"], st.at(0, 1, 1))
                    for i, src in ((3, maxA[:]), (2, maxB[:, :, 0:3]), (1, maxC[:])):
                        dve.tensor_reduce(rowmax[:, :, i:i + 1].rearrange("p h i -> p (h i)"), src, AX.X,
                                          ALU.max).then_inc(S["rowmax_ready"], 1)
                    dve.tensor_copy(rowmax[:, :, 0:1], maxB[:, :, 3:4]).then_inc(S["rowmax_ready"], 1)

                def body(st):
                    for g in range(NQUAD):
                        for item in plan(g):
                            if item.startswith("max") and st.has(max_stage(int(item[3:]))):
                                if item == "max0" and not st.first(2):
                                    dve.wait_ge(S["rowmax_ready"], st.at(1, 4, 4))
                                take_max(st, int(item[3:]))
                            elif item in STAGE and st.has(STAGE[item]):
                                job(st, item)

                steps(dve, body)


def routing_constants():
    before = bf16_bits(np.triu(np.ones((P, P), np.float32), 1))
    rank = np.arange(NE, 0, -1, dtype=np.float32)
    slot_row = np.repeat(np.arange(NSLOT, dtype=np.float32) % CSLOT * P, NE - 1).reshape(NSLOT, NE - 1)
    return before, rank, slot_row


SHARED, ROUTED = "shared", "routed"
LEAD = 3
NORM_LAG = 3


class Segment:

    def __init__(self, kind, first, count, base, mix_chunk, mix_at, every):
        self.kind, self.first, self.count, self.base = kind, first, count, base
        self.mix_chunk, self.mix_at, self.every = mix_chunk, mix_at, every
        mixed = mix_at + every * (CT + NORM_LAG) if mix_chunk is not None else 0
        self.steps = range(-LEAD, max(count + 2, mixed))
        self.turn = TURN * every

    def stages(self, n):
        mixing, token = self.mix_chunk is not None, (n - self.mix_at) // self.every
        return (tuple(0 <= n + off < self.count for off in (3, 1, 0, -1, -2)) + (n - 2 >= TURN,)
                + tuple(mixing and 0 <= token - off < CT for off in (0, 1, NORM_LAG))
                + (mixing and token >= NORM_LAG + TURN,))


SEGMENTS = []
for _kind, _first, _count, _chunk, _at, _every in (
        (SHARED, 0, CT, None, 0, 1), (ROUTED, 0, CSLOT, None, 0, 1),
        (ROUTED, CSLOT, CSLOT, 0, 2, 2), (SHARED, CT, CT, 1, 3, 1)):
    _base = SEGMENTS[-1].base + SEGMENTS[-1].count if SEGMENTS else 0
    SEGMENTS.append(Segment(_kind, _first, _count, _base, _chunk, _at, _every))


class TileStep:

    def __init__(self, seg, passed, like):
        self.seg, self.passed, self.like = seg, passed, like
        self.number = (passed if seg.every == 1 else passed * seg.every) + like

    def has(self, off):
        return 0 <= self.like + off < self.seg.count

    def ring(self, off, depth):
        return (self.like + off) % depth

    def mixes(self, off):
        turn, rest = divmod(self.like - self.seg.mix_at, self.seg.every)
        return self.seg.mix_chunk is not None and rest == 0 and 0 <= turn - off < CT

    def token(self, off):
        return self.passed + ((self.like - self.seg.mix_at) // self.seg.every - off)

    def token_ring(self, off, depth):
        return ((self.like - self.seg.mix_at) // self.seg.every - off) % depth

    def tile(self, off):
        return self.number + off + self.seg.base


def run_segments(eng, body, segments):
    for seg in segments:
        n = seg.steps.start
        while n < seg.steps.stop:
            run = n
            while run < seg.steps.stop and seg.stages(run) == seg.stages(n):
                run += 1
            turns = (run - n) // seg.turn
            if turns >= 2:
                with eng.Fori(0, TURN * (turns - 1) + 1, TURN) as passed:
                    for k in range(seg.turn):
                        body(TileStep(seg, passed, n + k))
                n += seg.turn * turns
            for k in range(n, run):
                body(TileStep(seg, 0, k))
            n = run


def experts(nc, io, dram, keep):
    with ExitStack() as ctx:
        def sb(name, shape, dt=F32):
            return ctx.enter_context(nc.sbuf_tensor("e_" + name, shape, dt))

        def ps(name):
            return ctx.enter_context(nc.psum_tensor("e_" + name, [P, T], F32))

        def sem(name):
            return ctx.enter_context(nc.semaphore("e_" + name))

        x1, logits, rank = keep["x1"], keep["logits"], keep["rank"]
        ident = sb("ident", [P, P])
        before = sb("before", [P, P], BF16)
        onesb = sb("onesb", [P, P], BF16)
        slot_row = sb("slot_row", [1, NSLOT, NE - 1])
        raw_in = [sb("raw_gate", [P, NE + 1, NCH, C]), sb("raw_up", [P, NE + 1, NCH, C])]
        raw_down = sb("raw_down", [P, NE + 1, F])
        w_in = sb("w_in", [P, NE + 1, 2, 2, F], F32R)
        w_down = sb("w_down", [P, NE + 1, NCH, C])
        top = [sb("best", [P, NTILE]), sb("second", [P, NTILE])]
        keyed = sb("keyed", [P, NTILE, NE])
        top_key = sb("top_key", [P, NTILE])
        one_both = sb("one_both", [P, 2 * NTILE * NE])
        one = [one_both[:, n * NTILE * NE:(n + 1) * NTILE * NE].rearrange("p (t e) -> p t e", e=NE) for n in range(2)]
        others = sb("others", [P, NTILE, NE])
        chosen = sb("chosen", [P, NTILE, NE], BF16)
        expo = sb("expo", [P, NTILE, NE])
        ratio = sb("ratio", [P, NTILE])
        norm = sb("norm", [P, NTILE])
        prob = [sb("prob_best", [P, NTILE]), sb("prob_second", [P, NTILE])]
        weight = [sb("weight_best", [P, NTILE]), sb("weight_second", [P, NTILE])]
        counts = sb("counts", [P, GROUPS, CT])
        running = sb("running", [P, GROUPS, CT])
        ones_f = sb("ones_f", [P, GROUPS * CT])
        start = sb("start", [P, GROUPS])
        group_n = sb("group_n", [P, GROUPS])
        group_i = sb("group_i", [P, GROUPS], I32)
        padded = sb("padded", [P, GROUPS])
        ends = sb("ends", [P, GROUPS])
        shift = sb("shift", [P, GROUPS])
        place = sb("place", [P, NTILE, NE])
        place_f = sb("place_f", [P, NTILE])
        place_i = [sb("place_best", [P, NTILE], I32), sb("place_second", [P, NTILE], I32)]
        past = one_both[0:1, 0:NSLOT * (NE - 1)].rearrange("p (s e) -> p s e", e=NE - 1)
        expert_f = sb("expert_f", [1, NSLOT])
        expert_i = sb("expert_i", [1, NSLOT], I32)
        total = sb("total", [P, NTILE, C])
        xs = sb("xs", [P, TURN, C])
        xT = [sb(f"xT{n}", [P, 2, P], F32R) for n in range(2)]
        gate = [sb(f"gate{n}", [P, F]) for n in range(2)]
        hid = [sb(f"hid{n}", [P, NCH * P]) for n in range(2)]
        hT = [t[:].rearrange("p g t -> p (g t)")[:, 0:NCH * P] for t in (counts, running)]
        after_raw = raw_down[:].rearrange("p e f -> p (e f)")[:, 0:5 * TURN * C].rearrange("p (n c) -> p n c", c=C)
        ys = after_raw[:, 0:TURN]
        picked = after_raw[:, TURN:3 * TURN].rearrange("p (s n) c -> p s n c", n=2)
        mixed = after_raw[:, 3 * TURN:4 * TURN]
        result = after_raw[:, 4 * TURN:5 * TURN]
        stats = sb("stats", [P, TURN, 6])
        mean_var = sb("mean_var", [P, TURN, 2])
        var_eps = sb("var_eps", [P, TURN])
        minus_half = sb("minus_half", [P, 1])
        rstd = sb("rstd", [P, TURN])

        gate_ps = [ps(f"gate_ps{n}") for n in range(2)]
        up_ps = [ps(f"up_ps{n}") for n in range(2)]
        x_ps, h_ps, y_ps, spare_ps = ps("x_ps"), ps("h_ps"), ps("y_ps"), ps("spare_ps")
        prep_ps = [gate_ps[0], up_ps[0], gate_ps[1], up_ps[1]]

        names = """const_loaded shared_loaded experts_loaded const_set weight_ps weight_kept routed prefix_ps exponents
            x_scattered0 x_scattered1 weight_rest x_ready xT_kept xT_rest gate_ready up_ready silu_done hid_done h_ready hT_kept
            y_ready y_taken half_set stats_passed mix_half mixed stats_taken aggregated stats_ready rstd_ready result_ready""".split()
        S = {n: sem(n) for n in names}
        xs_loaded = [sem(f"xs_loaded{n}") for n in range(TURN)]
        y_stored = [[sem(f"y{c}_stored{n}") for n in range(TURN)] for c in range(CHUNKS)]
        picked_in = [sem(f"picked_in{n}") for n in range(TURN)]
        out_stored = [sem(f"out_stored{n}") for n in range(TURN)]
        CONSTS, SHARED_RAWS, EXPERT_RAWS = 16 * 3, 16 * (2 * NCH + 1), 16 * (2 * NCH + 2)
        first_tiles, later_tiles = SEGMENTS[:1], SEGMENTS[1:]
        at_routed = {}
        STORED = 16 * (CSLOT // TURN)

        with nc.Block() as block:

            @block.vector
            def _(dve):
                done = [0]

                def link(ins, name=None):
                    done[0] += 1
                    ins.then_inc(S["routed"], 1)
                    dve.wait_ge(S["routed"], done[0])
                    if name:
                        at_routed[name] = done[0]

                dve.memset(onesb[:], 1.0).then_inc(S["const_set"], 1)
                dve.memset(ones_f[:], 1.0).then_inc(S["const_set"], 1)
                for n in range(2):
                    dve.memset(hid[n][:, F:], 0.0).then_inc(S["const_set"], 1)
                dve.wait_ge(S["const_set"], 4)
                by_expert = [P, NTILE, NE]

                link(dve.tensor_reduce(top[0][:], logits[:], AX.X, ALU.max))
                for n, src in ((0, logits), (1, others)):
                    link(dve.tensor_tensor(keyed[:], src[:], top[n][:].unsqueeze(2).to_broadcast(by_expert), ALU.is_equal))
                    link(dve.tensor_tensor(keyed[:], keyed[:], rank[:].unsqueeze(1).to_broadcast(by_expert), ALU.mult))
                    link(dve.tensor_reduce(top_key[:], keyed[:], AX.X, ALU.max))
                    link(dve.tensor_tensor(one[n], keyed[:], top_key[:].unsqueeze(2).to_broadcast(by_expert), ALU.is_equal))
                    if n == 0:
                        link(dve.scalar_tensor_tensor(others[:], one[0], NEG, logits[:], ALU.mult, ALU.add))
                        link(dve.tensor_reduce(top[1][:], others[:], AX.X, ALU.max))
                link(dve.tensor_tensor(chosen[:], one[0], one[1], ALU.add), "chosen")

                dve.wait_ge(S["prefix_ps"], 2)
                link(dve.tensor_copy(counts[:].rearrange("p (k e) t -> p k e t", k=CHUNKS),
                                     x_ps[:].rearrange("p (k t e) -> p k e t", k=CHUNKS, e=NE)), "counted")
                link(dve.tensor_tensor_scan(running[:].rearrange("p g t -> p (g t)"), ones_f[:],
                                            counts[:].rearrange("p g t -> p (g t)"), 0.0, ALU.mult, ALU.add))
                link(dve.tensor_tensor(start[:], running[:, :, 0], counts[:, :, 0], ALU.subtract))
                link(dve.tensor_tensor(group_n[:], running[:, :, CT - 1], start[:], ALU.subtract))
                link(dve.tensor_scalar(group_i[:], group_n[:], float(P - 1), None, ALU.add))
                tile_bits = P.bit_length() - 1
                link(dve.tensor_scalar(group_i[:], group_i[:], tile_bits, tile_bits,
                                       ALU.logical_shift_right, ALU.logical_shift_left))
                link(dve.tensor_copy(padded[:], group_i[:]))
                for c in range(CHUNKS):
                    g = slice(c * NE, (c + 1) * NE)
                    link(dve.tensor_tensor_scan(ends[:, g], ones_f[:, 0:NE], padded[:, g], 0.0,
                                                ALU.mult, ALU.add))
                link(dve.tensor_tensor(shift[:], ends[:], padded[:], ALU.subtract))
                link(dve.tensor_tensor(shift[:], shift[:], start[:], ALU.subtract))
                link(dve.tensor_tensor(running[:], running[:], counts[:], ALU.subtract))
                link(dve.tensor_tensor(running[:], running[:], shift[:].unsqueeze(2).to_broadcast([P, GROUPS, CT]), ALU.add))
                for c in range(CHUNKS):
                    tiles = slice(c * CT, (c + 1) * CT)
                    link(dve.tensor_tensor(place[:, tiles, :],
                                           spare_ps[:, c * CT * NE:(c + 1) * CT * NE].rearrange("p (t e) -> p t e", e=NE),
                                           running[:, c * NE:(c + 1) * NE, :].rearrange("p e t -> p t e"), ALU.add))
                for n in range(2):
                    link(dve.tensor_tensor(keyed[:], one[n], place[:], ALU.mult))
                    link(dve.tensor_reduce(place_f[:], keyed[:], AX.X, ALU.add))
                    link(dve.tensor_copy(place_i[n][:], place_f[:]), "placed")

                banks = [0]

                def keep_rests(e):
                    for w in range(2):
                        bank = prep_ps[(banks[0] + w) % len(prep_ps)]
                        dve.wait_ge(S["weight_kept"], banks[0] + w + 1)
                        dve.tensor_tensor(w_in[:, e, w, 1, :], bank[:, 0:F], w_in[:, e, w, 0, :].bitcast(F32),
                                          ALU.subtract).then_inc(S["weight_rest"], 1)
                    banks[0] += 3

                keep_rests(NE)

                def body(st):
                    seg = st.seg
                    if st.has(0):
                        k = st.ring(0, 2)
                        dve.wait_ge(S["silu_done"], st.tile(0) + 1)
                        dve.wait_ge(S["up_ready"], st.tile(0) + 1)
                        dve.tensor_tensor(hid[k][:, 0:F], gate[k][:], up_ps[k][:, 0:F], ALU.mult).then_inc(S["hid_done"], 1)
                    if st.has(1):
                        k = st.ring(1, 2)
                        dve.wait_ge(S["xT_kept"], st.tile(1) + 1)
                        dve.tensor_tensor(xT[k][:, 1, :], x_ps[:, 0:P], xT[k][:, 0, :].bitcast(F32),
                                          ALU.subtract).then_inc(S["xT_rest"], 1)
                    if seg.kind == SHARED and st.has(-2):
                        at = st.number - 2 + seg.first
                        dve.wait_ge(S["y_ready"], st.tile(-2) + 1)
                        dve.tensor_tensor(total[:, bass.ds(at, 1), :], y_ps[:, 0:C].unsqueeze(1),
                                          x1[:, bass.ds(at, 1), :], ALU.add).then_inc(S["y_taken"], 1)
                    def where(off):
                        return st.token_ring(off, TURN), st.token(off) + seg.mix_chunk * CT

                    def add_choice(n):
                        slot, tile = where(0)
                        dve.scalar_tensor_tensor(mixed[:, slot:slot + 1, :], picked[:, slot, n:n + 1, :],
                                                 weight[n][:, bass.ds(tile, 1)],
                                                 mixed[:, slot:slot + 1, :] if n else total[:, bass.ds(tile, 1), :],
                                                 ALU.mult, ALU.add).then_inc(S["mixed" if n else "mix_half"], 1)

                    if st.mixes(0):
                        slot, tile = where(0)
                        dve.wait_ge(picked_in[slot], (tile - slot) * (32 // TURN) + 32)
                        dve.wait_ge(S["y_taken"], (seg.base if seg.mix_chunk else 0) + st.token(0) + 1)
                        add_choice(0)
                    if st.mixes(NORM_LAG):
                        slot, tile = where(NORM_LAG)
                        dve.wait_ge(S["rstd_ready"], tile + 1)
                        if (st.like - seg.mix_at) // seg.every - NORM_LAG >= TURN or seg.mix_chunk:
                            dve.wait_ge(out_stored[slot], (tile - slot) * (16 // TURN))
                        dve.tensor_scalar(result[:, slot, :], mixed[:, slot, :], mean_var[:, slot, 0:1],
                                          rstd[:, slot:slot + 1], ALU.subtract, ALU.mult).then_inc(S["result_ready"], 1)
                    if st.mixes(0):
                        dve.wait_ge(S["mix_half"], where(0)[1] + 1)
                        add_choice(1)
                    if st.mixes(1):
                        slot, tile = where(1)
                        dve.wait_ge(S["stats_taken"], tile + 1)
                        dve.sem_inc(S["stats_passed"], 1)
                        dve.bn_aggr(mean_var[:, slot, :], stats[:, slot, :]).then_inc(S["aggregated"], 1)
                    if st.mixes(0):
                        slot, tile = where(0)
                        dve.wait_ge(S["mixed"], tile + 1)
                        dve.bn_stats(stats[:, slot, :], mixed[:, slot, :]).then_inc(S["stats_taken"], 1)
                    if st.mixes(1):
                        slot, tile = where(1)
                        dve.wait_ge(S["aggregated"], tile + 1)
                        dve.tensor_scalar(var_eps[:, slot:slot + 1], mean_var[:, slot, 1:2], EPS, None,
                                          ALU.add).then_inc(S["stats_ready"], 1)

                run_segments(dve, body, first_tiles)

                link(dve.tensor_tensor(expo[:], logits[:], top[0][:].unsqueeze(2).to_broadcast(by_expert), ALU.subtract))
                link(dve.tensor_tensor(ratio[:], top[1][:], top[0][:], ALU.subtract), "exponents")
                for e in range(NE):
                    keep_rests(e)

                dve.wait_ge(S["const_loaded"], CONSTS)
                for c in range(CHUNKS):
                    s = slice(c * CSLOT, (c + 1) * CSLOT)
                    link(dve.tensor_tensor(past[:, s, :], slot_row[:, s, :],
                                           ends[0:1, c * NE:(c + 1) * NE - 1].unsqueeze(1).to_broadcast([1, CSLOT, NE - 1]),
                                           ALU.is_ge))
                link(dve.tensor_reduce(expert_f[:], past, AX.X, ALU.add))
                link(dve.tensor_copy(expert_i[:], expert_f[:]), "experts")

                dve.wait_ge(S["exponents"], 2)
                link(dve.tensor_reduce(norm[:], expo[:], AX.X, ALU.add))
                link(dve.reciprocal(prob[0][:], norm[:]))
                link(dve.tensor_tensor(prob[1][:], ratio[:], prob[0][:], ALU.mult))
                link(dve.tensor_tensor(norm[:], prob[0][:], prob[1][:], ALU.add))
                link(dve.tensor_scalar(norm[:], norm[:], 1e-20, None, ALU.add))
                link(dve.reciprocal(norm[:], norm[:]))
                for n in range(2):
                    link(dve.tensor_tensor(weight[n][:], prob[n][:], norm[:], ALU.mult))

                run_segments(dve, body, later_tiles)

            @block.sync
            def _(sp):
                for raw, name in zip(raw_in, ("gate", "up")):
                    for j, (f0, fw) in enumerate(FCH):
                        sp.dma_start(raw[0:fw, NE, j, :], io["shared_" + name][f0:f0 + fw, :]).then_inc(S["shared_loaded"], 16)
                sp.dma_start(raw_down[:, NE, :], io["shared_down"]).then_inc(S["shared_loaded"], 16)
                for out, in_ in ((ident[:], io["ident"]), (before[:].bitcast(U16), io["before"]),
                                 (slot_row[:], io["slot_row"].unsqueeze(0))):
                    sp.dma_start(out, in_).then_inc(S["const_loaded"], 16)

                def body(st):
                    seg = st.seg
                    chunk = seg.first // CSLOT
                    if st.has(3):
                        if seg.kind == ROUTED and st.like == -3:
                            sp.wait_ge(S[f"x_scattered{chunk}"], 32 * CT)
                        slot, n = st.ring(3, TURN), st.number + 3
                        if seg.base or st.like + 3 >= TURN:
                            sp.wait_ge(S["x_ready"], st.tile(3) + 1 - TURN)
                        src = x1[:, bass.ds(n + seg.first, 1), :] if seg.kind == SHARED else \
                            dram["x_sorted"][chunk][bass.ds(n * P, P), :].unsqueeze(1)
                        sp.dma_start(xs[:, slot:slot + 1, :], src).then_inc(xs_loaded[slot], 16)
                    if seg.kind == ROUTED and st.has(-2):
                        slot, n = st.ring(-2, TURN), st.number - 2
                        sp.wait_ge(S["y_taken"], st.tile(-2) + 1)
                        sp.dma_start(dram["y_sorted"][chunk][bass.ds(n * P, P), :], ys[:, slot, :]).then_inc(y_stored[chunk][slot], 16)
                    if st.mixes(NORM_LAG):
                        slot, n = st.token_ring(NORM_LAG, TURN), st.token(NORM_LAG) + seg.mix_chunk * CT
                        sp.wait_ge(S["result_ready"], n + 1)
                        sp.dma_start(dram["out"][bass.ds(n * P, P), :], result[:, slot, :]).then_inc(out_stored[slot], 16)

                run_segments(sp, body, SEGMENTS)
                for slot in range(TURN):
                    sp.wait_ge(out_stored[slot], 16 * NTILE // TURN)

            @block.tensor
            def _(pe):
                pe.wait_ge(S["const_loaded"], CONSTS)
                banks = [0]

                def transpose_weights(e):
                    for w in range(3):
                        n = banks[0]
                        if n >= len(prep_ps):
                            full, w_before = divmod(n - len(prep_ps), 3)
                            pe.wait_ge(S["weight_kept"], n - len(prep_ps) + 1)
                            pe.wait_ge(S["weight_rest"], 2 * full + min(w_before + 1, 2))
                        bank = prep_ps[n % len(prep_ps)]
                        for j, (f0, fw) in enumerate(FCH):
                            if w < 2:
                                last = pe.transpose(bank[:, f0:f0 + fw], raw_in[w][0:fw, e, j, :], ident[0:fw, 0:fw])
                            else:
                                last = pe.transpose(bank[0:fw, j * C:(j + 1) * C], raw_down[:, e, f0:f0 + fw], ident[:])
                        last.then_inc(S["weight_ps"], 1)
                        banks[0] += 1

                pe.wait_ge(S["const_set"], 4)
                pe.wait_ge(S["routed"], at_routed["chosen"])
                tokens = chosen[:].rearrange("p t e -> p (t e)")
                pe.matmul(spare_ps[:], before[:], tokens, start=True, stop=True).then_inc(S["prefix_ps"], 1)
                pe.matmul(x_ps[:], onesb[:], tokens, start=True, stop=True).then_inc(S["prefix_ps"], 1)
                pe.wait_ge(S["shared_loaded"], SHARED_RAWS)
                transpose_weights(NE)
                pe.wait_ge(S["weight_kept"], banks[0])
                pe.wait_ge(S["weight_rest"], banks[0] // 3 * 2)
                pe.wait_ge(S["routed"], at_routed["counted"])
                expert_of = [ctx.enter_context(pe.register(f"expert_of{n}")) for n in range(TURN)]

                def load_expert(st, off):
                    pe.reg_load(expert_of[st.ring(off, TURN)],
                                expert_i[0:1, bass.ds(st.number + off + st.seg.first, 1)])

                def expert(st, off):
                    if st.seg.kind == SHARED:
                        return slice(NE, NE + 1)
                    return bass.ds(pe.snap(expert_of[st.ring(off, TURN)], min_val=0, max_val=NE - 1), 1)

                def body(st):
                    seg = st.seg
                    if st.has(0):
                        k, e = st.ring(0, 2), expert(st, 0)
                        pe.wait_ge(S["xT_rest"], st.tile(0) + 1)
                        for w, (bank, done) in enumerate(((gate_ps[k], "gate_ready"), (up_ps[k], "up_ready"))):
                            for n, (x_part, w_part) in enumerate(((0, 0), (0, 1), (1, 0))):
                                last = pe.matmul(bank[:, 0:F], xT[k][:, x_part, :],
                                                 w_in[:, e, w, w_part, :].rearrange("p a f -> p (a f)"),
                                                 start=n == 0, stop=n == 2)
                            last.then_inc(S[done], 1)
                    if seg.kind == ROUTED and st.has(1):
                        load_expert(st, 1)
                    if st.has(1):
                        slot = st.ring(1, TURN)
                        pe.wait_ge(xs_loaded[slot], (st.tile(1) - slot) * (16 // TURN) + 16)
                        pe.transpose(x_ps[:, 0:P], xs[:, slot, :], ident[:]).then_inc(S["x_ready"], 1)
                    if st.has(-1):
                        k = st.ring(-1, 2)
                        pe.wait_ge(S["hid_done"], st.tile(-1) + 1)
                        if seg.base or st.like >= 2:
                            pe.wait_ge(S["hT_kept"], st.tile(-1))
                        for j in range(NCH):
                            last = pe.transpose(h_ps[:, j * P:(j + 1) * P], hid[k][:, j * P:(j + 1) * P], ident[:])
                        last.then_inc(S["h_ready"], 1)
                    if st.has(-2):
                        k, e = st.ring(-2, 2), expert(st, -2)
                        if not st.has(-1):
                            pe.wait_ge(S["hT_kept"], st.tile(-2) + 1)
                        if seg.base or st.like >= 3:
                            pe.wait_ge(S["y_taken"], st.tile(-2))
                        for j, (f0, fw) in enumerate(FCH):
                            last = pe.matmul(y_ps[:, 0:C], hT[k][0:fw, j * P:(j + 1) * P],
                                             w_down[0:fw, e, j, :].rearrange("p a c -> p (a c)"),
                                             start=j == 0, stop=j == NCH - 1)
                        last.then_inc(S["y_ready"], 1)

                run_segments(pe, body, first_tiles)
                pe.wait_ge(S["experts_loaded"], EXPERT_RAWS)
                for e in range(NE):
                    transpose_weights(e)
                pe.wait_ge(S["weight_kept"], banks[0])
                pe.wait_ge(S["weight_rest"], banks[0] // 3 * 2)
                pe.wait_ge(S["routed"], at_routed["experts"])
                run_segments(pe, body, later_tiles)

            @block.scalar
            def _(act):
                act.wait_ge(S["shared_loaded"], SHARED_RAWS)
                for raw, name in zip(raw_in, ("gate", "up")):
                    for j, (f0, fw) in enumerate(FCH):
                        act.dma_start(raw[0:fw, 0:NE, j, :], io["expert_" + name][:, f0:f0 + fw, :]
                                      .rearrange("e p c -> p e c")).then_inc(S["experts_loaded"], 16)
                for e in range(0, NE, NE // 2):
                    act.dma_start(raw_down[:, e:e + NE // 2, :], io["expert_down"][e:e + NE // 2]
                                  .rearrange("e c f -> c e f")).then_inc(S["experts_loaded"], 16)
                banks = [0]

                def keep_weights(e):
                    for w in range(3):
                        act.wait_ge(S["weight_ps"], banks[0] + 1)
                        bank = prep_ps[banks[0] % len(prep_ps)]
                        if w < 2:
                            last = act.activation(w_in[:, e, w, 0, :], bank[:, 0:F], ACT.Copy)
                        else:
                            act.activation(w_down[:, e, 0:NCH - 1, :].rearrange("p a c -> p (a c)"),
                                           bank[:, 0:(NCH - 1) * C], ACT.Copy)
                            rows = FCH[-1][1]
                            last = act.activation(w_down[0:rows, e, NCH - 1, :],
                                                  bank[0:rows, (NCH - 1) * C:NCH * C], ACT.Copy)
                        last.then_inc(S["weight_kept"], 1)
                        banks[0] += 1

                keep_weights(NE)
                def body(st):
                    if st.has(0):
                        k = st.ring(0, 2)
                        act.wait_ge(S["gate_ready"], st.tile(0) + 1)
                        act.activation(gate[k][:], gate_ps[k][:, 0:F], ACT.Silu).then_inc(S["silu_done"], 1)
                    if st.has(1):
                        act.wait_ge(S["x_ready"], st.tile(1) + 1)
                        act.activation(xT[st.ring(1, 2)][:, 0, :], x_ps[:, 0:P], ACT.Copy).then_inc(S["xT_kept"], 1)
                    if st.has(-1):
                        act.wait_ge(S["h_ready"], st.tile(-1) + 1)
                        act.activation(hT[st.ring(-1, 2)], h_ps[:, 0:NCH * P], ACT.Copy).then_inc(S["hT_kept"], 1)
                    if st.seg.kind == ROUTED and st.has(-2):
                        chunk, slot = st.seg.first // CSLOT, st.ring(-2, TURN)
                        act.wait_ge(S["y_ready"], st.tile(-2) + 1)
                        if st.like - 2 >= TURN:
                            act.wait_ge(y_stored[chunk][slot], (st.number - 2 - slot) * (16 // TURN))
                        elif chunk:
                            act.wait_ge(y_stored[chunk - 1][slot], STORED)
                        act.activation(ys[:, slot, :], y_ps[:, 0:C], ACT.Copy).then_inc(S["y_taken"], 1)

                run_segments(act, body, first_tiles)
                act.wait_ge(S["routed"], at_routed["exponents"])
                for t in (expo[:].rearrange("p t e -> p (t e)"), ratio[:]):
                    act.activation(t, t, ACT.Exp).then_inc(S["exponents"], 1)
                for e in range(NE):
                    keep_weights(e)
                run_segments(act, body, later_tiles)

            @block.gpsimd
            def _(pool):
                pool.memset(minus_half[:], -0.5).then_inc(S["half_set"], 1)
                pool.wait_ge(S["half_set"], 1)
                pool.wait_ge(S["routed"], at_routed["placed"])
                for c in range(CHUNKS):
                    for t in range(c * CT, (c + 1) * CT):
                        for n in range(2):
                            pool.indirect_dma_start(out=dram["x_sorted"][c],
                                                    out_offset=bass.IndirectOffsetOnAxis(ap=place_i[n][:, t:t + 1], axis=0),
                                                    in_=x1[:, t, :], in_offset=None).then_inc(S[f"x_scattered{c}"], 16)

                def gather(t):
                    for n in range(2):
                        pool.indirect_dma_start(out=picked[:, t % TURN, n, :], out_offset=None, in_=dram["y_sorted"][t // CT],
                                                in_offset=bass.IndirectOffsetOnAxis(ap=place_i[n][:, t:t + 1], axis=0)) \
                            .then_inc(picked_in[t % TURN], 16)

                for c in range(CHUNKS):
                    for slot in range(TURN):
                        pool.wait_ge(y_stored[c][slot], STORED)
                    for t in range(c * CT, c * CT + TURN):
                        gather(t)
                    for t in range(c * CT, (c + 1) * CT):
                        slot = t % TURN
                        pool.wait_ge(S["stats_ready"], t + 1)
                        pool.tensor_tensor(rstd[:, slot:slot + 1], var_eps[:, slot:slot + 1], minus_half[:],
                                           ALU.pow).then_inc(S["rstd_ready"], 1)
                        if t + TURN < (c + 1) * CT:
                            gather(t + TURN)


_INPUTS = {"x": "L0_attn_x", "q_w": "L0_attn_q_w", "q_b": "L0_attn_q_b", "kv_w": "L0_attn_kv_w", "kv_b": "L0_attn_kv_b",
           "o_w": "L0_attn_o_w", "o_b": "L0_attn_o_b", "gate_w": "L0_ffn_gate_w", "expert_gate": "L0_ffn_expert_gate",
           "expert_up": "L0_ffn_expert_up", "expert_down": "L0_ffn_expert_down", "shared_gate": "L0_ffn_shared_gate",
           "shared_up": "L0_ffn_shared_up", "shared_down": "L0_ffn_shared_down"}


def constants():
    q, k = stack_constants()
    before, rank, slot_row = routing_constants()
    eye = np.eye(P, dtype=np.float32)
    return {"ident": eye, "identb": bf16_bits(eye), "causal": causal_constant(), "qstack_rows": q,
            "kstack_rows": k, "before": before, "rank": rank, "slot_row": slot_row}


def build(nc, io):
    dram = {"out": io["out"],
            "parts": [nc.dram_tensor(f"parts{n}", (2, PARTS, HD, NH, T), BF16).ap() for n in range(2)],
            "x_sorted": [nc.dram_tensor(f"x_sorted{c}", (CSLOT * P, C), F32).ap() for c in range(CHUNKS)],
            "y_sorted": [nc.dram_tensor(f"y_sorted{c}", (CSLOT * P, C), F32).ap() for c in range(CHUNKS)]}
    with nc.sbuf_tensor("x1_all", [P, NTILE, C], F32) as x1, nc.sbuf_tensor("logits", [P, NTILE, NE], F32) as logits, \
            nc.sbuf_tensor("rank", [P, NE], F32) as rank:
        keep = {"x1": x1, "logits": logits, "rank": rank}
        attention(nc, io, dram, keep)
        experts(nc, io, dram, keep)


def kernel(**inputs):
    import concourse.bacc as bacc
    from concourse.bass_utils import run_bass_kernel_spmd

    nc = bacc.Bacc("TRN2", target_bir_lowering=False, num_devices=1)
    arrays = {n: np.ascontiguousarray(inputs[source]) for n, source in _INPUTS.items()} | constants()
    io = {n: nc.dram_tensor("in_" + n, a.shape, mybir.dt.from_np(a.dtype), kind="ExternalInput").ap()
          for n, a in arrays.items()}
    io["out"] = nc.dram_tensor("out", (B * T, C), F32, kind="ExternalOutput").ap()
    build(nc, io)
    said = run_bass_kernel_spmd(nc, [{"in_" + n: a for n, a in arrays.items()}], core_ids=[0])
    return np.asarray(said.results[0]["out"]).reshape(B, T, C)
```
